# Optimizing a Trainium2 kernel written in Bass

```python
import numpy as np
import jax
import jax.numpy as jnp

def _softmax(x, axis=-1):
    return jax.nn.softmax(x, axis=axis)

def _gelu(x):
    return jax.nn.gelu(x, approximate=True)

def _silu(x):
    return jax.nn.silu(x)

def _sigmoid(x):
    return jax.nn.sigmoid(x)

def _layernorm(x, axis=-1, eps=1e-05):
    m = jnp.mean(x, axis=axis, keepdims=True)
    v = jnp.var(x, axis=axis, keepdims=True)
    return (x - m) / jnp.sqrt(v + eps)

def _scatter_add(tgt, idx, src, axis=0):
    return tgt.at[idx].add(src)

def _segment_sum(src, seg, n):
    return jax.ops.segment_sum(src, seg, n)
kernel_name = 'mk_macaron_d1_jaxref_r8_fb1567'

def setup_inputs(seed: int=0):
    np.random.seed(seed)
    _w = jnp.asarray

    def _L0_attn_setup():
        import math
        import jax, jax.numpy as jnp
        import numpy as np
        from jax import lax
        D_MODEL = 128
        N_LAYERS = 2
        D_STATE = 16
        D_CONV = 4
        EXPAND = 2
        D_INNER = EXPAND * D_MODEL
        DT_RANK = math.ceil(D_MODEL / 16)
        BATCH = 2
        SEQLEN = 128
        BETA = 0.6
        ALPHA = 1.0
        EPS = 1e-05
        DT_MIN, DT_MAX, DT_FLOOR = (0.001, 0.1, 0.0001)

        def _rmsnorm(x, w):
            return x * jax.lax.rsqrt(jnp.mean(x * x, axis=-1, keepdims=True) + EPS) * w

        def _block(x, in_w, cw, cb, xp_w, dtw, dtb, a_log, dp, ow):
            B, L, _ = x.shape
            xz = jnp.einsum('bld,ed->ble', x, in_w)
            xb, z = jnp.split(xz, 2, axis=-1)
            xc = lax.conv_general_dilated(xb.transpose(0, 2, 1), cw[:, None, :], window_strides=(1,), padding=[(D_CONV - 1, 0)], dimension_numbers=('NCH', 'OIH', 'NCH'), feature_group_count=D_INNER)
            xb = jax.nn.silu((xc + cb[None, :, None]).transpose(0, 2, 1))
            dbc = jnp.einsum('ble,re->blr', xb, xp_w)
            delta = dbc[..., :DT_RANK]
            Bm = dbc[..., DT_RANK:DT_RANK + D_STATE]
            Cm = dbc[..., DT_RANK + D_STATE:]
            delta = jax.nn.softplus(jnp.einsum('blr,er->ble', delta, dtw) + dtb)
            dA = jnp.exp(delta[..., None] * -jnp.exp(a_log))
            mi = ALPHA * delta[..., None] * Bm[:, :, None, :] * xb[..., None]

            def scan_fn(carry, inp):
                h, v = carry
                dA_t, mi_t, C_t = inp
                v = BETA * v + mi_t
                h = dA_t * h + v
                y_t = jnp.einsum('ben,bn->be', h, C_t)
                return ((h, v), y_t)
            h0 = jnp.zeros((B, D_INNER, D_STATE), dtype=x.dtype)
            _, ys = lax.scan(scan_fn, (h0, h0), (dA.transpose(1, 0, 2, 3), mi.transpose(1, 0, 2, 3), Cm.transpose(1, 0, 2)))
            y = ys.transpose(1, 0, 2) + dp * xb
            y = y * jax.nn.silu(z)
            return jnp.einsum('ble,de->bld', y, ow)
        key = jax.random.key(seed)
        ks = jax.random.split(key, 10)
        std = 0.02
        nl = N_LAYERS
        x = jax.random.normal(ks[0], (BATCH, SEQLEN, D_MODEL), dtype=jnp.float32)
        in_proj_w = jax.random.normal(ks[1], (nl, 2 * D_INNER, D_MODEL), dtype=jnp.float32) * std
        conv_w = jax.random.normal(ks[2], (nl, D_INNER, D_CONV), dtype=jnp.float32) * std
        conv_b = jnp.zeros((nl, D_INNER), dtype=jnp.float32)
        x_proj_w = jax.random.normal(ks[3], (nl, DT_RANK + 2 * D_STATE, D_INNER), dtype=jnp.float32) * std
        dt_std = DT_RANK ** (-0.5)
        dt_w = jax.random.uniform(ks[4], (nl, D_INNER, DT_RANK), dtype=jnp.float32, minval=-dt_std, maxval=dt_std)
        dt = jnp.exp(jax.random.uniform(ks[5], (nl, D_INNER), dtype=jnp.float32) * (math.log(DT_MAX) - math.log(DT_MIN)) + math.log(DT_MIN))
        dt = jnp.clip(dt, DT_FLOOR, None)
        dt_b = dt + jnp.log(-jnp.expm1(-dt))
        A_log = jnp.broadcast_to(jnp.log(jnp.arange(1, D_STATE + 1, dtype=jnp.float32)), (nl, D_INNER, D_STATE)).copy()
        Dp = jnp.ones((nl, D_INNER), dtype=jnp.float32)
        out_w = jax.random.normal(ks[6], (nl, D_MODEL, D_INNER), dtype=jnp.float32) * std
        norm_w = jnp.ones((nl, D_MODEL), dtype=jnp.float32)
        return {'x': x, 'norm_w': norm_w, 'in_proj_w': in_proj_w, 'conv_w': conv_w, 'conv_b': conv_b, 'x_proj_w': x_proj_w, 'dt_w': dt_w, 'dt_b': dt_b, 'A_log': A_log, 'Dp': Dp, 'out_w': out_w}
    _L0_attn_in = _L0_attn_setup()

    def _L0_ffn_setup():
        import jax, jax.numpy as jnp
        import numpy as np
        ALPHA = 1.5
        TEMP = 1.0
        N_ITER = 25
        THRESH = 1e-09

        def entmax_bisect(X, alpha=ALPHA, n_iter=N_ITER):
            d = X.shape[-1]
            inv_am1 = 1.0 / (alpha - 1.0)
            Xs = X * (alpha - 1.0)
            max_val = jnp.max(Xs, axis=-1, keepdims=True)
            tau_lo = max_val - 1.0
            tau_hi = max_val - (1.0 / d) ** (alpha - 1.0)
            f_lo = jnp.sum(jnp.maximum(Xs - tau_lo, 0.0) ** inv_am1, axis=-1, keepdims=True) - 1.0

            def body(i, carry):
                tau_lo, dm, _ = carry
                dm = dm * 0.5
                tau_m = tau_lo + dm
                f_m = jnp.sum(jnp.maximum(Xs - tau_m, 0.0) ** inv_am1, axis=-1, keepdims=True) - 1.0
                tau_lo = jnp.where(f_m * f_lo >= 0.0, tau_m, tau_lo)
                return (tau_lo, dm, tau_m)
            dm0 = tau_hi - tau_lo
            _, _, tau_m = jax.lax.fori_loop(0, n_iter, body, (tau_lo, dm0, tau_lo))
            p = jnp.maximum(Xs - tau_m, 0.0) ** inv_am1
            return p / jnp.sum(p, axis=-1, keepdims=True)
        key = jax.random.key(seed)
        ks = jax.random.split(key, 8)
        B, S, D, E = (2, 128, 128, 8)
        F = 4 * D
        return {'x': jax.random.normal(ks[0], (B, S, D), jnp.float32), 'Wr': jax.random.normal(ks[1], (D, E), jnp.float32) * 0.02, 'br': jnp.zeros((E,), jnp.float32), 'W1': jax.random.normal(ks[2], (E, D, F), jnp.float32) * 0.02, 'b1': jnp.zeros((E, F), jnp.float32), 'W2': jax.random.normal(ks[3], (E, F, D), jnp.float32) * 0.02, 'b2': jnp.zeros((E, D), jnp.float32)}
    _L0_ffn_in = _L0_ffn_setup()
    _d = {'L0_attn_x': _L0_attn_in['x'], 'L0_attn_norm_w': _L0_attn_in['norm_w'], 'L0_attn_in_proj_w': _L0_attn_in['in_proj_w'], 'L0_attn_conv_w': _L0_attn_in['conv_w'], 'L0_attn_conv_b': _L0_attn_in['conv_b'], 'L0_attn_x_proj_w': _L0_attn_in['x_proj_w'], 'L0_attn_dt_w': _L0_attn_in['dt_w'], 'L0_attn_dt_b': _L0_attn_in['dt_b'], 'L0_attn_A_log': _L0_attn_in['A_log'], 'L0_attn_Dp': _L0_attn_in['Dp'], 'L0_attn_out_w': _L0_attn_in['out_w'], 'L0_ffn_Wr': _L0_ffn_in['Wr'], 'L0_ffn_br': _L0_ffn_in['br'], 'L0_ffn_W1': _L0_ffn_in['W1'], 'L0_ffn_b1': _L0_ffn_in['b1'], 'L0_ffn_W2': _L0_ffn_in['W2'], 'L0_ffn_b2': _L0_ffn_in['b2']}
    _x0 = _d['L0_attn_x']
    _d['L0_attn_x'] = jax.random.normal(jax.random.fold_in(jax.random.key(seed), 1), (4, 512, 128), dtype=_x0.dtype)
    del _x0
    return _d

def reference(L0_attn_x, L0_attn_norm_w, L0_attn_in_proj_w, L0_attn_conv_w, L0_attn_conv_b, L0_attn_x_proj_w, L0_attn_dt_w, L0_attn_dt_b, L0_attn_A_log, L0_attn_Dp, L0_attn_out_w, L0_ffn_Wr, L0_ffn_br, L0_ffn_W1, L0_ffn_b1, L0_ffn_W2, L0_ffn_b2):

    def _L0_attn_ref(x, norm_w, in_proj_w, conv_w, conv_b, x_proj_w, dt_w, dt_b, A_log, Dp, out_w):
        import math
        import jax, jax.numpy as jnp
        import numpy as np
        from jax import lax
        D_MODEL = 128
        N_LAYERS = 2
        D_STATE = 16
        D_CONV = 4
        EXPAND = 2
        D_INNER = EXPAND * D_MODEL
        DT_RANK = math.ceil(D_MODEL / 16)
        BATCH = 2
        SEQLEN = 128
        BETA = 0.6
        ALPHA = 1.0
        EPS = 1e-05
        DT_MIN, DT_MAX, DT_FLOOR = (0.001, 0.1, 0.0001)

        def _rmsnorm(x, w):
            return x * jax.lax.rsqrt(jnp.mean(x * x, axis=-1, keepdims=True) + EPS) * w

        def _block(x, in_w, cw, cb, xp_w, dtw, dtb, a_log, dp, ow):
            B, L, _ = x.shape
            xz = jnp.einsum('bld,ed->ble', x, in_w)
            xb, z = jnp.split(xz, 2, axis=-1)
            xc = lax.conv_general_dilated(xb.transpose(0, 2, 1), cw[:, None, :], window_strides=(1,), padding=[(D_CONV - 1, 0)], dimension_numbers=('NCH', 'OIH', 'NCH'), feature_group_count=D_INNER)
            xb = jax.nn.silu((xc + cb[None, :, None]).transpose(0, 2, 1))
            dbc = jnp.einsum('ble,re->blr', xb, xp_w)
            delta = dbc[..., :DT_RANK]
            Bm = dbc[..., DT_RANK:DT_RANK + D_STATE]
            Cm = dbc[..., DT_RANK + D_STATE:]
            delta = jax.nn.softplus(jnp.einsum('blr,er->ble', delta, dtw) + dtb)
            dA = jnp.exp(delta[..., None] * -jnp.exp(a_log))
            mi = ALPHA * delta[..., None] * Bm[:, :, None, :] * xb[..., None]

            def scan_fn(carry, inp):
                h, v = carry
                dA_t, mi_t, C_t = inp
                v = BETA * v + mi_t
                h = dA_t * h + v
                y_t = jnp.einsum('ben,bn->be', h, C_t)
                return ((h, v), y_t)
            h0 = jnp.zeros((B, D_INNER, D_STATE), dtype=x.dtype)
            _, ys = lax.scan(scan_fn, (h0, h0), (dA.transpose(1, 0, 2, 3), mi.transpose(1, 0, 2, 3), Cm.transpose(1, 0, 2)))
            y = ys.transpose(1, 0, 2) + dp * xb
            y = y * jax.nn.silu(z)
            return jnp.einsum('ble,de->bld', y, ow)
        for i in range(N_LAYERS):
            x = x + _block(_rmsnorm(x, norm_w[i]), in_proj_w[i], conv_w[i], conv_b[i], x_proj_w[i], dt_w[i], dt_b[i], A_log[i], Dp[i], out_w[i])
        return x

    def _L0_ffn_ref(x, Wr, br, W1, b1, W2, b2):
        import jax, jax.numpy as jnp
        import numpy as np
        ALPHA = 1.5
        TEMP = 1.0
        N_ITER = 25
        THRESH = 1e-09

        def entmax_bisect(X, alpha=ALPHA, n_iter=N_ITER):
            d = X.shape[-1]
            inv_am1 = 1.0 / (alpha - 1.0)
            Xs = X * (alpha - 1.0)
            max_val = jnp.max(Xs, axis=-1, keepdims=True)
            tau_lo = max_val - 1.0
            tau_hi = max_val - (1.0 / d) ** (alpha - 1.0)
            f_lo = jnp.sum(jnp.maximum(Xs - tau_lo, 0.0) ** inv_am1, axis=-1, keepdims=True) - 1.0

            def body(i, carry):
                tau_lo, dm, _ = carry
                dm = dm * 0.5
                tau_m = tau_lo + dm
                f_m = jnp.sum(jnp.maximum(Xs - tau_m, 0.0) ** inv_am1, axis=-1, keepdims=True) - 1.0
                tau_lo = jnp.where(f_m * f_lo >= 0.0, tau_m, tau_lo)
                return (tau_lo, dm, tau_m)
            dm0 = tau_hi - tau_lo
            _, _, tau_m = jax.lax.fori_loop(0, n_iter, body, (tau_lo, dm0, tau_lo))
            p = jnp.maximum(Xs - tau_m, 0.0) ** inv_am1
            return p / jnp.sum(p, axis=-1, keepdims=True)
        B, S, D = x.shape
        xt = x.reshape(B * S, D)
        logits = (xt @ Wr + br) / TEMP
        gates = entmax_bisect(logits)
        gates = jnp.where(gates > THRESH, gates, 0.0)
        h = jax.nn.relu(jnp.einsum('td,edf->etf', xt, W1) + b1[:, None, :])
        y = jnp.einsum('etf,efd->etd', h, W2) + b2[:, None, :]
        out = jnp.einsum('etd,te->td', y, gates)
        return out.reshape(B, S, D)
    x = L0_attn_x
    x = x + 0.5 * _L0_ffn_ref(_layernorm(x, axis=-1), L0_ffn_Wr, L0_ffn_br, L0_ffn_W1, L0_ffn_b1, L0_ffn_W2, L0_ffn_b2)
    x = x + _L0_attn_ref(_layernorm(x, axis=-1), L0_attn_norm_w, L0_attn_in_proj_w, L0_attn_conv_w, L0_attn_conv_b, L0_attn_x_proj_w, L0_attn_dt_w, L0_attn_dt_b, L0_attn_A_log, L0_attn_Dp, L0_attn_out_w)
    x = x + 0.5 * _L0_ffn_ref(_layernorm(x, axis=-1), L0_ffn_Wr, L0_ffn_br, L0_ffn_W1, L0_ffn_b1, L0_ffn_W2, L0_ffn_b2)
    return x

_drawn_inputs = setup_inputs


def setup_inputs(seed=0):
    import zlib

    import numpy as np

    out = dict(_drawn_inputs(seed))
    spreads = {'L0_attn_norm_w': (1.0, 0.6),
     'L0_attn_conv_b': (0.0, 0.8),
     'L0_attn_Dp': (1.0, 0.6),
     'L0_ffn_br': (0.0, 0.561),
     'L0_ffn_b1': (0.0, 0.8),
     'L0_ffn_b2': (0.0, 0.271)}
    factors = {'L0_attn_in_proj_w': 8.0,
     'L0_attn_conv_w': 8.0,
     'L0_attn_x_proj_w': 8.0,
     'L0_attn_dt_w': 8.0,
     'L0_attn_dt_b': 8.0,
     'L0_attn_A_log': 8.0,
     'L0_attn_out_w': 8.0,
     'L0_ffn_Wr': 2.791,
     'L0_ffn_W1': 2.826}
    for name, (base, spread) in spreads.items():
        noise = np.random.default_rng([zlib.crc32(name.encode()), seed]).standard_normal(out[name].shape)
        drawn = base * np.exp(spread * noise) if base else spread * noise
        out[name] = jnp.asarray(drawn.astype(out[name].dtype))
    for name, factor in factors.items():
        out[name] = (out[name] * factor).astype(out[name].dtype)
    return out
```

```python
from contextlib import ExitStack

import concourse.bass as bass
import numpy as np
from concourse import mybir

F32 = mybir.dt.float32
ALU = mybir.AluOpType
ACT = mybir.ActivationFunctionType
AX = mybir.AxisListType
TABLES = "natural_log_exp_and_others"

D = 128
NB = 4
L = 512
E = 8
F = 512
FT = F // 128
S1 = E * FT
TT = L // 128
EI = 256
ET = EI // 128
NS = 16
R = 8
KC = 4
NL = 2
CH = 64
NC = L // CH
UN = NC * ET
CW = NS * CH
HC = NC // 2
BETA = 0.6
EPS = 1e-5
ITERS = 25
SMALL = 1.0 / 32

PACK = [("in_w", 2 * EI), ("xp", ET * (R + 2 * NS)), ("out_w", ET * D), ("conv_w", ET * KC), ("conv_b", ET),
        ("dt_b", ET), ("a_log", ET * NS), ("dp", ET), ("norm_w", 1), ("dt_w", EI)]
COL, NW = {}, 0
for _name, _n in PACK:
    COL[_name] = NW
    NW += _n


class Ffn:

    def __init__(self, nc, x, src, out, dram, consts, tag):
        self.nc, self.x, self.src, self.out, self.dram, self.tag = nc, x, src, out, dram, tag
        self.consts = consts

    def build(self):
        nc, x, tag = self.nc, self.x, self.tag
        with ExitStack() as ctx:
            def sb(name, shape):
                return ctx.enter_context(nc.sbuf_tensor(f"{name}_{tag}", shape, F32))

            def sem(name):
                return ctx.enter_context(nc.semaphore(f"{name}_{tag}"))

            ps = ctx.enter_context(nc.psum_tensor(f"ps_{tag}", [128, 8, 512], F32))
            ps_hidden = [ps[:, 0, :], ps[:, 1, :]]
            ps_y = [ps[:, 2, :], ps[:, 3, :]]
            ps_gate = ps[:, 4, :]
            ps_logit = ps[:, 7, 0:NB * TT * E]
            ps_gT = ps[0:E, 5, :]

            w1 = sb("w1", [D, S1, 128])
            w2 = sb("w2", [128, S1, D])
            b1 = sb("b1", [128, S1])
            b2 = sb("b2", [D, E])
            wr = sb("wr", [D, E])
            br = sb("br", [128, E])
            ones = sb("ones", [128, 128])
            ident = sb("ident", [128, 128])
            sel = sb("sel", [E, E, 128])
            eps = sb("eps", [128, 1])
            xn = sb("xn", [D, NB, L])
            hidden = sb("hidden", [128, 4, L])
            yb = sb("yb", [D, E, L])
            prod = sb("prod", [D, L])
            acc = sb("acc", [D, L])
            G = NB * TT
            xs = sb("xs", [128, G, E])
            z = sb("z", [128, G, E])
            z2 = sb("z2", [128, G, E])
            gates = sb("gates", [128, G, E])
            mask = sb("mask", [128, G, E])
            mx = sb("mx", [128, G])
            lo = sb("lo", [128, G])
            dm = sb("dm", [128, G])
            tau = sb("tau", [128, G])
            f_lo = sb("f_lo", [128, G])
            f_m = sb("f_m", [128, G])
            step = sb("step", [128, G])
            gT = sb("gT", [E, NB * L])

            s_x = sem("x_loaded")
            s_c = sem("constants_loaded")
            s_w1 = [sem(f"w1_{e}_loaded") for e in range(E)]
            s_w2 = [sem(f"w2_{e}_loaded") for e in range(E)]
            s_mean = sem("mean_ready")
            s_xc = sem("centred_ready")
            s_sq = sem("squares_ready")
            s_var = sem("variance_ready")
            s_lnv = sem("log_variance_ready")
            s_rs = sem("rstd_ready")
            s_xn = sem("normed_ready")
            s_log = sem("logits_ready")
            s_dve = sem("gating_step_done")
            s_exp = sem("gating_log_done")
            s_gates = sem("gates_ready")
            s_gt = sem("gates_transposed")
            s_gtc = sem("gates_copied")
            s_gb = sem("gate_broadcast")
            s_mm1 = sem("hidden_product_ready")
            s_h = sem("hidden_ready")
            s_mm2 = sem("hidden_used")
            s_y = sem("expert_output_ready")
            s_prod = sem("gated_output_ready")
            s_acc = sem("gated_sum_ready")
            s_new = sem("x_updated")
            s_out = sem("x_stored")
            s_passed = sem("wait_passed")
            LAG = 2

            with nc.Block() as block:
                @block.sync
                def _(sp):
                    if self.src is not None:
                        sp.dma_start(x[:, :, :], self.src).then_inc(s_x, 16)
                    for t, name in ((b1, "b1"), (b2, "b2"), (wr, "wr"), (ones, "ones"), (ident, "ident"), (sel, "sel"), (br, "br")):
                        src = self.dram[name]
                        sp.dma_start(t[tuple([slice(None)] * len(t.shape))], src).then_inc(s_c, 16)
                    for e in range(E):
                        sp.dma_start(w1[:, e * FT:(e + 1) * FT, :], self.dram["w1"][:, e * FT:(e + 1) * FT, :]).then_inc(s_w1[e], 16)
                        sp.dma_start(w2[:, e * FT:(e + 1) * FT, :], self.dram["w2"][:, e * FT:(e + 1) * FT, :]).then_inc(s_w2[e], 16)
                    if self.out is not None:
                        for c in range(NB):
                            sp.wait_ge(s_new, c + 1)
                            sp.dma_start(self.out[:, c, :], x[:, c, :]).then_inc(s_out, 16)
                        sp.wait_ge(s_out, 16 * NB)

                @block.tensor
                def _(pe):
                    if self.src is not None:
                        pe.wait_ge(s_x, 16)
                    pe.wait_ge(s_c, 16 * 7)
                    for c in range(NB):
                        pe.matmul(ps[:, c, :], ones[:, :], x[:, c, :], start=True, stop=True).then_inc(s_mean, 1)
                    for c in range(NB):
                        pe.wait_ge(s_sq, c + 1)
                        pe.matmul(ps[:, NB + c, :], ones[:, :], hidden[:, c, :], start=True, stop=True).then_inc(s_var, 1)
                    pe.wait_ge(s_xn, NB)
                    for t in range(NB * TT):
                        mm = pe.matmul(ps_logit[:, t * E:(t + 1) * E], xn[:, t // TT, (t % TT) * 128:(t % TT + 1) * 128], wr[:, :],
                                       start=True, stop=True)
                    mm.then_inc(s_log, 1)

                    def hidden_product(c, s):
                        if isinstance(c, int) and c == 0 and s % FT == 0:
                            pe.wait_ge(s_w1[s // FT], 16)
                        if not (isinstance(c, int) and c == 0 and s < 2):
                            pe.wait_ge(s_h, c * S1 + s - 1)
                        pe.matmul(ps_hidden[s % 2], w1[:, s, :], xn[:, bass.ds(c, 1), :], start=True, stop=True).then_inc(s_mm1, 1)

                    def expert_product(c, s):
                        e, f = s // FT, s % FT
                        if isinstance(c, int) and c == 0 and f == 0:
                            pe.wait_ge(s_w2[e], 16)
                        if f == 0 and not (isinstance(c, int) and c == 0 and e < 2):
                            pe.wait_ge(s_y, c * E + e - 1)
                        pe.wait_ge(s_h, c * S1 + s + 1)
                        mm = pe.matmul(ps_y[e % 2], w2[:, s, :], hidden[:, s % 4, :], start=(f == 0), stop=(f == FT - 1))
                        mm.then_inc(s_mm2, 1)

                    def gate_broadcast(c, e):
                        pe.wait_ge(s_prod, c * E + e + 1)
                        pe.sem_inc(s_passed, 1)
                        pe.matmul(ps_gate, sel[:, e, :], gT[:, bass.ds(c * L, L)], start=True, stop=True).then_inc(s_gb, 1)

                    def batch(c, gates_of):
                        for s in range(S1 + LAG):
                            if s < S1:
                                if gates_of is not None and s % FT == 0:
                                    gate_broadcast(gates_of, s // FT)
                                hidden_product(c, s)
                            if s >= LAG:
                                expert_product(c, s - LAG)

                    batch(0, None)
                    pe.wait_ge(s_gates, 1)
                    for c in range(NB):
                        if c:
                            pe.wait_ge(s_gtc, c)
                        for t in range(TT):
                            mm = pe.transpose(ps_gT[:, t * 128:(t + 1) * 128], gates[:, c * TT + t, :], ident[:, :])
                        mm.then_inc(s_gt, 1)
                    pe.wait_ge(s_gtc, NB)
                    with pe.Fori(1, NB) as c:
                        batch(c, c - 1)
                    for e in range(E):
                        gate_broadcast(NB - 1, e)

                @block.scalar
                def _(act):
                    act.preload_act_table_set(TABLES)
                    act.wait_ge(s_c, 16 * 7)
                    for c in range(NB):
                        act.wait_ge(s_xc, c + 1)
                        act.activation(hidden[:, c, :], yb[:, c, :], ACT.Square).then_inc(s_sq, 1)
                    for c in range(NB):
                        act.wait_ge(s_var, c + 1)
                        act.activation(yb[:, NB + c, :], ps[:, NB + c, :], ACT.Ln, bias=eps[:, 0:1]).then_inc(s_lnv, 1)
                    for c in range(NB):
                        act.wait_ge(s_lnv, c + 1)
                        act.activation(yb[:, NB + c, :], yb[:, NB + c, :], ACT.Exp, scale=-0.5).then_inc(s_rs, 1)

                    def relu(c, s):
                        act.wait_ge(s_mm1, c * S1 + s + 1)
                        if not (isinstance(c, int) and c == 0 and s < 4):
                            act.wait_ge(s_mm2, c * S1 + s - 3)
                        act.activation(hidden[:, s % 4, :], ps_hidden[s % 2], ACT.Relu, bias=b1[:, s:s + 1]).then_inc(s_h, 1)

                    def expert_out(c, e):
                        act.wait_ge(s_mm2, c * S1 + (e + 1) * FT)
                        if not (isinstance(c, int) and c == 0):
                            act.wait_ge(s_prod, (c - 1) * E + e + 2)
                        act.activation(yb[:, e, :], ps_y[e % 2], ACT.Identity, bias=b2[:, e:e + 1]).then_inc(s_y, 1)

                    def batch(c):
                        for s in range(S1 + LAG + 1):
                            if s < S1:
                                relu(c, s)
                            if s > LAG and (s - LAG - 1) % FT == FT - 1:
                                expert_out(c, (s - LAG - 1) // FT)

                    batch(0)
                    with act.Fori(1, NB) as c:
                        batch(c)

                @block.vector
                def _(dve):
                    dve.sem_inc(s_prod, 1)
                    dve.memset(eps[:, :], EPS).then_inc(s_dve, 1)
                    for c in range(NB):
                        dve.wait_ge(s_mean, c + 1)
                        dve.tensor_tensor(yb[:, c, :], x[:, c, :], ps[:, c, :], ALU.subtract).then_inc(s_xc, 1)
                    for c in range(NB):
                        dve.wait_ge(s_xc, c + 1)
                        dve.wait_ge(s_rs, c + 1)
                        dve.tensor_tensor(xn[:, c, :], yb[:, c, :], yb[:, NB + c, :], ALU.mult).then_inc(s_xn, 1)

                    done = [1]

                    def then(ins):
                        done[0] += 1
                        ins.then_inc(s_dve, 1)
                        dve.wait_ge(s_dve, done[0])

                    def wide(t):
                        return t[:, :].unsqueeze(2).broadcast_to([128, G, E])

                    def power_sum(out, tau_ap):
                        then(dve.tensor_tensor(z[:, :, :], xs[:, :, :], tau_ap, ALU.subtract))
                        then(dve.scalar_tensor_tensor(z2[:, :, :], z[:, :, :], 0.0, z[:, :, :], ALU.max, ALU.mult))
                        then(dve.tensor_reduce(out[:, :], z2[:, :, :], AX.X, ALU.add))

                    dve.wait_ge(s_log, 1)
                    dve.wait_ge(s_c, 16 * 7)
                    lg = ps_logit.rearrange("p (g e) -> p g e", e=E)
                    then(dve.tensor_tensor(z[:, :, :], lg, br[:, :].unsqueeze(1).broadcast_to([128, G, E]), ALU.add))
                    then(dve.tensor_scalar(xs[:, :, :], z[:, :, :], 0.5, None, ALU.mult))
                    then(dve.tensor_reduce(mx[:, :], xs[:, :, :], AX.X, ALU.max))
                    then(dve.tensor_scalar(lo[:, :], mx[:, :], -1.0, None, ALU.add))
                    then(dve.tensor_scalar(dm[:, :], mx[:, :], -float(np.float32((1.0 / E) ** 0.5)), None, ALU.add))
                    then(dve.tensor_tensor(dm[:, :], dm[:, :], lo[:, :], ALU.subtract))
                    power_sum(f_lo, wide(lo))
                    then(dve.tensor_scalar(f_lo[:, :], f_lo[:, :], -1.0, None, ALU.add))
                    for k in range(ITERS):
                        half = 0.5 ** (k + 1)
                        then(dve.scalar_tensor_tensor(tau[:, :], dm[:, :], half, lo[:, :], ALU.mult, ALU.add))
                        power_sum(f_m, wide(tau))
                        if k < ITERS - 1:
                            then(dve.scalar_tensor_tensor(step[:, :], f_m[:, :], -1.0, f_lo[:, :], ALU.add, ALU.mult))
                            then(dve.scalar_tensor_tensor(step[:, :], step[:, :], 0.0, dm[:, :], ALU.is_ge, ALU.mult))
                            then(dve.scalar_tensor_tensor(lo[:, :], step[:, :], half, lo[:, :], ALU.mult, ALU.add))
                    then(dve.reciprocal(step[:, :], f_m[:, :]))
                    then(dve.tensor_tensor(z[:, :, :], z2[:, :, :], wide(step), ALU.mult))
                    dve.scalar_tensor_tensor(gates[:, :, :], z[:, :, :], 1e-9, z[:, :, :], ALU.is_gt, ALU.mult).then_inc(s_gates, 1)
                    for c in range(NB):
                        dve.wait_ge(s_gt, c + 1)
                        dve.tensor_copy(gT[:, c * L:(c + 1) * L], ps_gT).then_inc(s_gtc, 1)

                    def combine(c):
                        for e in range(E):
                            dve.wait_ge(s_gb, c * E + e + 1)
                            dve.wait_ge(s_y, c * E + e + 1)
                            if e == 0:
                                if not isinstance(c, int):
                                    dve.wait_ge(s_new, c)
                                dve.tensor_tensor(acc[:, :], yb[:, e, :], ps_gate, ALU.mult).then_inc(s_prod, 1)
                                continue
                            if e > 1:
                                dve.wait_ge(s_acc, c * (E - 1) + e - 1)
                            dve.tensor_tensor(prod[:, :], yb[:, e, :], ps_gate, ALU.mult).then_inc(s_prod, 1)
                            dve.wait_ge(s_prod, c * E + e + 2)
                            dve.tensor_tensor(acc[:, :], acc[:, :], prod[:, :], ALU.add).then_inc(s_acc, 1)
                        dve.wait_ge(s_acc, (c + 1) * (E - 1))
                        dve.scalar_tensor_tensor(x[:, bass.ds(c, 1), :], acc[:, :].unsqueeze(1), 0.5, x[:, bass.ds(c, 1), :], ALU.mult, ALU.add)\
                           .then_inc(s_new, 1)

                    combine(0)
                    with dve.Fori(1, NB) as c:
                        combine(c)


class Mamba:

    def __init__(self, nc, x, dram):
        self.nc, self.x, self.dram = nc, x, dram

    def build(self):
        nc, x, dram = self.nc, self.x, self.dram
        with ExitStack() as ctx:
            def sb(name, shape):
                return ctx.enter_context(nc.sbuf_tensor(name, shape, F32))

            def sem(name):
                return ctx.enter_context(nc.semaphore(name))

            ps = ctx.enter_context(nc.psum_tensor("ps_m", [128, 8, 512], F32))
            ps_v = [ps[:, 2 * et:2 * et + 2, :].rearrange("p b (n t) -> p (b n) t", t=CH) for et in range(ET)]
            ps_v_half = [[ps[:, 2 * et + b, :] for b in range(2)] for et in range(ET)]
            ps_uT = ps[0:CH, 4, 0:EI]
            ps_carry = ps[0:NS, 4, EI:2 * EI]
            bank_a, bank_b, bank_c = ps[:, 5, :], ps[:, 6, :], ps[:, 7, :]

            a = sb("a", [D, NB, L])
            wts = [sb(f"wts{p}", [128, NW]) for p in range(2)]
            ones = sb("ones_m", [128, 128])
            ident = sb("ident_m", [128, 128])
            kern = sb("kern", [CH, CH])
            zeros = sb("zeros", [NS, EI])
            eps = sb("eps_m", [128, 1])
            decay = sb("decay", [128, 2, ET, HC, NS, CH])
            decay0 = sb("decay0", [128, 2, ET, HC, NS])
            cb = sb("cb", [128, NC, NS, CH])
            g = [sb(f"g{p}", [CH + NS, NS, CH]) for p in range(2)]
            su = [sb(f"su{p}", [CH + NS, EI]) for p in range(2)]
            h = [sb(f"h{et}", [128, NS, CH]) for et in range(ET)]
            hc = [sb(f"hc{k}", [128, NS, CH]) for k in range(4)]
            carry_in = sb("carry_in", [128, NS])
            sq = sb("sq_m", [D, L])
            rs = sb("rs_m", [D, L])
            xr = sb("xr", [D, L])
            cv = [sb(f"cv{et}", [128, KC - 1 + L]) for et in range(ET)]
            conv = sb("conv", [128, L])
            sig = sb("sig", [128, L])
            xb = [sb(f"xb{p}", [128, ET, L]) for p in range(2)]
            sz = [sb(f"sz{p}", [128, ET, L]) for p in range(2)]
            u = [sb(f"u{p}", [128, ET, L]) for p in range(2)]
            bt = [sb(f"bt{p}", [CH, NC, NS]) for p in range(2)]
            dtc = sb("dtc", [32 + NS, L])
            dtr, csb = dtc[0:R, :], dtc[32:32 + NS, :]
            mag, ex, lg, lin = sq, rs, xr, conv
            delta = sb("delta", [128, ET, L])
            aexp = sb("aexp", [128, ET * NS])
            aneg = [sb(f"aneg{p}", [128, ET * NS]) for p in range(2)]
            y = sb("y", [128, ET, L])

            ln_x, ln_sq, ln_rs = (lambda c, t=t: t[c // ET][:, c % ET, :] for t in (u, sz, xb))

            s_c = sem("m_constants_loaded")
            s_init = sem("m_fills_done")
            s_eps = sem("m_eps_filled")
            s_wt = [sem(f"m_weights{p}_loaded") for p in range(2)]
            s_mean = sem("m_mean_ready")
            s_lnx = sem("m_centred_ready")
            s_lnsq = sem("m_ln_squares_ready")
            s_lnvar = sem("m_ln_variance_ready")
            s_lnlog = sem("m_ln_log_ready")
            s_lnrs = sem("m_ln_rstd_ready")
            s_a = sem("m_layernorm_ready")
            s_sq = sem("m_squares_ready")
            s_ms = sem("m_mean_square_ready")
            s_log = sem("m_log_ready")
            s_rs = sem("m_rstd_ready")
            s_xr = sem("m_normed_ready")
            s_xi = sem("m_inner_product_ready")
            s_z = sem("m_gate_product_ready")
            s_cv = sem("m_inner_copied")
            s_sa = sem("m_act_sigmoid_step")
            s_szs = sem("m_gate_sigmoid_ready")
            s_sz = sem("m_gate_silu_ready")
            s_cd = sem("m_conv_step")
            s_cs = sem("m_conv_sigmoid_ready")
            s_xb = sem("m_inner_silu_ready")
            s_xp = sem("m_x_products_ready")
            s_xpc = sem("m_x_products_copied")
            s_dtp = sem("m_dt_product_ready")
            s_mag = sem("m_dt_magnitude_ready")
            s_ex = sem("m_dt_exp_ready")
            s_sp = sem("m_dt_log_and_relu_ready")
            s_sd = sem("m_softplus_step")
            s_delta = sem("m_delta_ready")
            s_u = sem("m_u_ready")
            s_al = sem("m_a_exp_ready")
            s_an = sem("m_a_ready")
            s_da = sem("m_decay_ready")
            s_d0 = sem("m_decay0_ready")
            s_d0c = sem("m_decay0_copied")
            s_cst = sem("m_c_stored")
            s_cb = [sem(f"m_c{c}_spread") for c in range(NC)]
            s_g = sem("m_kernel_ready")
            s_uT = sem("m_uT_ready")
            s_ca = sem("m_carry_product_ready")
            s_su = sem("m_scan_inputs_ready")
            s_v = sem("m_v_ready")
            s_t0 = sem("m_carry_step")
            s_scan = sem("m_scan_done")
            s_hc = sem("m_hc_ready")
            s_y = sem("m_y_reduced")
            s_yd = sem("m_y_skip_added")
            s_yg = sem("m_y_gated")
            s_op = sem("m_out_product_ready")
            s_res = sem("m_residual_added")
            s_end = sem("m_x_updated")
            s_passed = {name: sem(f"m_wait_passed_{name}") for name in ("pe", "pool", "sp", "dve")}

            def w(p, name, k=0, n=1, rows=128):
                at = COL[name] + k
                return wts[p][0:rows, at:at + n]

            def is0(i):
                return isinstance(i, int) and i == 0

            def bodies(eng, prepare, chunk, finish, open_=None):
                def body(i, p, more):
                    for c in range(NC):
                        chunk(i, p, c, more)
                        if more:
                            prepare(i + 1, 1 - p, c)
                    finish(i, p)

                for c in range(NC):
                    prepare(0, 0, c)
                if open_ is not None:
                    open_()
                body(0, 0, True)
                with eng.Fori(0, NL * NB // 2 - 1) as j:
                    body(j * 2 + 1, 1, True)
                    body(j * 2 + 2, 0, True)
                body(NL * NB - 1, 1, False)

            with nc.Block() as block:
                @block.sync
                def _(sp):
                    for t, name in ((ones, "ones"), (ident, "ident"), (kern, "kern")):
                        sp.dma_start(t[:, :], dram[name]).then_inc(s_c, 16)
                    for p in range(2):
                        sp.dma_start(g[p][CH:CH + NS, :, :], dram["carry_kern"]).then_inc(s_c, 16)

                    def prepare(i, p, c):
                        if c == 0:
                            if isinstance(i, int):
                                if i >= 2:
                                    sp.wait_ge(s_res, i - 1)
                            elif p == 0:
                                sp.wait_ge(s_res, i - 1)
                            else:
                                sp.wait_ge(s_res, i - 1)
                            layer = i // NB
                            src = dram["mw"][layer, :, :] if isinstance(layer, int) else dram["mw"][bass.ds(layer, 1), :, :].rearrange("o p n -> (o p) n")
                            sp.dma_start(wts[p][:, :], src).then_inc(s_wt[p], 16)
                        if c == 3:
                            sp.wait_ge(s_xpc, i * 3 + 2)
                            sp.sem_inc(s_passed["sp"], 1)
                            if not is0(i):
                                for k in range(NC):
                                    sp.wait_ge(s_cb[k], i * 16)
                            sp.dma_start(dram["c_scratch"].rearrange("c n t -> n c t"),
                                         csb.rearrange("n (c t) -> n c t", t=CH)).then_inc(s_cst, 16)
                            sp.wait_ge(s_cst, i * 16 + 16)
                            sp.sem_inc(s_passed["sp"], 1)
                        if c >= 3:
                            for k in {3: [0, 1, 2], 4: [3], 5: [4], 6: [5], 7: [6, 7]}[c]:
                                if not is0(i):
                                    sp.wait_ge(s_hc, (i - 1) * UN + ET * (k + 1))
                                sp.dma_start(cb[:, k, :, :], dram["c_scratch"][k:k + 1, :, :].broadcast_to([128, NS, CH]))\
                                  .then_inc(s_cb[k], 16)

                    bodies(sp, prepare, lambda i, p, c, more: None, lambda i, p: None)

                @block.tensor
                def _(pe):
                    pe.wait_ge(s_c, 16 * 5)
                    for c in range(NB):
                        pe.matmul(ps[:, c, :], ones[:, :], x[:, c, :], start=True, stop=True).then_inc(s_mean, 1)
                    for c in range(NB):
                        pe.wait_ge(s_lnsq, c + 1)
                        pe.matmul(ps[:, NB + c, :], ones[:, :], ln_sq(c), start=True, stop=True).then_inc(s_lnvar, 1)

                    def transposes(i, p, c):
                        if not (is0(i) and c == 0):
                            pe.wait_ge(s_su, i * NC + c)
                        if c == 0:
                            pe.wait_ge(s_u, i * ET + ET)
                        pe.sem_inc(s_passed["pe"], 1)
                        for et in range(ET):
                            mm = pe.transpose(ps_uT[:, et * 128:(et + 1) * 128], u[p][:, et, c * CH:(c + 1) * CH], ident[:, :])
                        mm.then_inc(s_uT, 1)

                    def prepare(i, p, c):
                        if c == 0:
                            pe.wait_ge(s_sq, i + 1)
                            if is0(i):
                                pe.wait_ge(s_a, NB)
                            else:
                                pe.wait_ge(s_delta, i * ET)
                            pe.matmul(bank_a, ones[:, :], sq[:, :], start=True, stop=True).then_inc(s_ms, 1)
                            pe.wait_ge(s_wt[p], (i // 2) * 16 + 16 if isinstance(i, int) else (i >> 1) * 16 + 16)
                            pe.wait_ge(s_xr, i + 1)
                            pe.matmul(bank_b, w(p, "in_w", 0, 128), xr[:, :], start=True, stop=True).then_inc(s_xi, 1)
                            if not is0(i):
                                if isinstance(i, int):
                                    if i >= 2:
                                        pe.wait_ge(s_res, i - 1)
                                else:
                                    pe.wait_ge(s_res, i - 1)
                            pe.matmul(bank_c, w(p, "in_w", 128, 128), xr[:, :], start=True, stop=True).then_inc(s_xi, 1)
                            pe.matmul(bank_a, w(p, "in_w", EI, 128), xr[:, :], start=True, stop=True).then_inc(s_z, 1)
                            pe.wait_ge(s_cv, i * ET + 1)
                            pe.matmul(bank_b, w(p, "in_w", EI + 128, 128), xr[:, :], start=True, stop=True).then_inc(s_z, 1)
                        if c == 2:
                            pe.wait_ge(s_sz, i * ET + ET)
                            pe.wait_ge(s_xb, i * ET + ET)
                            for et in range(ET):
                                mm = pe.matmul(bank_c[0:R, :], w(p, "xp", et * (R + 2 * NS), R), xb[p][:, et, :], start=(et == 0), stop=(et == ET - 1))
                            mm.then_inc(s_xp, 1)
                            for et in range(ET):
                                mm = pe.matmul(bank_b[0:NS, :], w(p, "xp", et * (R + 2 * NS) + R + NS, NS), xb[p][:, et, :],
                                               start=(et == 0), stop=(et == ET - 1))
                            mm.then_inc(s_xp, 1)
                            for k in range(NC):
                                for et in range(ET):
                                    mm = pe.matmul(bank_a[0:CH, k * NS:(k + 1) * NS], xb[p][:, et, k * CH:(k + 1) * CH],
                                                   w(p, "xp", et * (R + 2 * NS) + R, NS), start=(et == 0), stop=(et == ET - 1))
                            mm.then_inc(s_xp, 1)
                            pe.wait_ge(s_xpc, i * 3 + 3)
                            for et, bank in ((0, bank_a), (1, bank_b)):
                                pe.matmul(bank, w(p, "dt_w", et * 128, 128, R), dtr, start=True, stop=True).then_inc(s_dtp, 1)

                    def chunk(i, p, c, more):
                        q = i * NC + c
                        pe.wait_ge(s_su, q + 1)
                        pe.wait_ge(s_g, q + 1)
                        for et in range(ET):
                            if not (is0(i) and c == 0):
                                pe.wait_ge(s_scan, (q - 1) * ET + et + 1)
                            for b in range(2):
                                mm = pe.matmul(ps_v_half[et][b], su[c % 2][:, et * 128:(et + 1) * 128],
                                               g[c % 2][:, b * NS // 2:(b + 1) * NS // 2, :], start=True, stop=True)
                            mm.then_inc(s_v, 1)
                        if c < NC - 1:
                            transposes(i, p, c + 1)
                            pe.matmul(ps_carry, g[c % 2][:, :, CH - 1], su[c % 2][:, :], start=True, stop=True).then_inc(s_ca, 1)
                        elif more:
                            transposes(i + 1, 1 - p, 0)

                    def finish(i, p):
                        for et in range(ET):
                            pe.wait_ge(s_yg, i * ET + et + 1)
                            mm = pe.matmul(bank_c, w(p, "out_w", et * D, D), y[:, et, :], start=(et == 0), stop=(et == ET - 1))
                        mm.then_inc(s_op, 1)

                    bodies(pe, prepare, chunk, finish, open_=lambda: transposes(0, 0, 0))

                @block.scalar
                def _(act):
                    act.preload_act_table_set(TABLES)
                    act.wait_ge(s_init, 3)
                    act.wait_ge(s_eps, 1)
                    for c in range(NB):
                        act.wait_ge(s_lnx, c + 1)
                        act.activation(ln_sq(c), ln_x(c), ACT.Square).then_inc(s_lnsq, 1)
                    for c in range(NB):
                        act.wait_ge(s_lnvar, c + 1)
                        act.activation(ln_rs(c), ps[:, NB + c, :], ACT.Ln, bias=eps[:, 0:1]).then_inc(s_lnlog, 1)
                    for c in range(NB):
                        act.wait_ge(s_lnlog, c + 1)
                        act.activation(ln_rs(c), ln_rs(c), ACT.Exp, scale=-0.5).then_inc(s_lnrs, 1)

                    def sigmoid(src, count):
                        act.activation(sig[:, :], src, ACT.Exp, scale=-1.0).then_inc(s_sa, 1)
                        act.wait_ge(s_sa, count + 1)
                        act.activation(sig[:, :], sig[:, :], ACT.Ln, bias=1.0).then_inc(s_sa, 1)
                        act.wait_ge(s_sa, count + 2)
                        return act.activation(sig[:, :], sig[:, :], ACT.Exp, scale=-1.0)

                    def decays(i, half, part):
                        et = part // 2
                        for n in range((part % 2) * NS // 2, (part % 2 + 1) * NS // 2):
                            ins = act.activation(decay[:, half, et, :, n, :],
                                                 delta[:, et, half * L // 2:(half + 1) * L // 2].rearrange("p (c t) -> p c t", t=CH),
                                                 ACT.Exp, scale=aneg_of[0][:, et * NS + n:et * NS + n + 1])
                        ins.then_inc(s_da, 1)

                    aneg_of = [aneg[0]]

                    def prepare(i, p, c):
                        if c == 0:
                            if is0(i):
                                act.wait_ge(s_a, NB)
                            else:
                                if isinstance(i, int):
                                    if i >= NB:
                                        act.wait_ge(s_res, i - NB + 1)
                                else:
                                    act.wait_ge(s_res, (i - 1) * 1)
                            if not is0(i):
                                act.wait_ge(s_delta, i * ET)
                            act.activation(sq[:, :].unsqueeze(1), a[:, bass.ds(i & (NB - 1), 1), :], ACT.Square).then_inc(s_sq, 1)
                            act.wait_ge(s_ms, i + 1)
                            act.activation(rs[:, :], bank_a, ACT.Ln, bias=eps[:, 0:1]).then_inc(s_log, 1)
                            act.wait_ge(s_log, i + 1)
                            act.activation(rs[:, :], rs[:, :], ACT.Exp, scale=-0.5).then_inc(s_rs, 1)
                            for et, bank in ((0, bank_b), (1, bank_c)):
                                act.wait_ge(s_xi, i * ET + et + 1)
                                act.activation(cv[et][:, KC - 1:KC - 1 + L], bank, ACT.Copy).then_inc(s_cv, 1)
                            act.wait_ge(s_wt[p], (i // 2) * 16 + 16 if isinstance(i, int) else (i >> 1) * 16 + 16)
                            act.activation(aexp[:, :], w(p, "a_log", 0, ET * NS), ACT.Exp).then_inc(s_al, 1)
                        if c == 1:
                            for et, bank in ((0, bank_a), (1, bank_b)):
                                if et:
                                    act.wait_ge(s_sz, i * ET + 1)
                                elif not is0(i):
                                    act.wait_ge(s_xb, i * ET)
                                act.wait_ge(s_z, i * ET + et + 1)
                                sigmoid(bank, (i * 2 * ET + et) * 2).then_inc(s_szs, 1)
                        if c == 2:
                            for et in range(ET):
                                act.wait_ge(s_sz, i * ET + ET)
                                if et:
                                    act.wait_ge(s_xb, i * ET + 1)
                                act.wait_ge(s_cd, (i * ET + et + 1) * KC)
                                sigmoid(conv[:, :], (i * 2 * ET + ET + et) * 2).then_inc(s_cs, 1)
                            act.wait_ge(s_xp, i * 3 + 1)
                            act.activation(dtr, bank_c[0:R, :], ACT.Copy).then_inc(s_xpc, 1)
                            act.wait_ge(s_xp, i * 3 + 2)
                            if not is0(i):
                                act.wait_ge(s_cst, i * 16)
                            act.activation(csb, bank_b[0:NS, :], ACT.Copy).then_inc(s_xpc, 1)
                            act.wait_ge(s_xp, i * 3 + 3)
                            act.activation(bt[p][:, :, :], bank_a[0:CH, 0:NC * NS].rearrange("p (c n) -> p c n", n=NS), ACT.Copy)\
                               .then_inc(s_xpc, 1)
                        if c == 3:
                            for et, bank in ((0, bank_a), (1, bank_b)):
                                act.wait_ge(s_dtp, i * ET + et + 1)
                                if et:
                                    act.wait_ge(s_delta, i * ET + et)
                                act.activation(mag[:, :], bank, ACT.Abs, bias=w(p, "dt_b", et)).then_inc(s_mag, 1)
                                act.wait_ge(s_mag, i * ET + et + 1)
                                act.activation(ex[:, :], mag[:, :], ACT.Exp, scale=-1.0).then_inc(s_ex, 1)
                                act.wait_ge(s_ex, i * ET + et + 1)
                                act.activation(lg[:, :], ex[:, :], ACT.Ln, bias=1.0).then_inc(s_sp, 1)
                                act.activation(lin[:, :], bank, ACT.Relu, bias=w(p, "dt_b", et)).then_inc(s_sp, 1)
                        if c >= HC:
                            aneg_of[0] = aneg[p]
                            if c == HC:
                                act.wait_ge(s_delta, i * ET + ET)
                                act.wait_ge(s_an, i + 1)
                                if not is0(i):
                                    act.wait_ge(s_scan, (i - 1) * UN + UN // 2)
                            decays(i, 0, c - HC)

                    def scan_inputs(i, p, c):
                        act.wait_ge(s_uT, i * NC + c + 1)
                        if c:
                            act.wait_ge(s_ca, i * (NC - 1) + c)
                        act.activation(su[c % 2][0:CH, :], ps_uT, ACT.Copy)
                        if c == 0:
                            ins = act.activation(su[0][CH:CH + NS, :], zeros[:, :], ACT.Copy)
                        else:
                            ins = act.activation(su[c % 2][CH:CH + NS, :], ps_carry, ACT.Copy)
                        ins.then_inc(s_su, 1)

                    def chunk(i, p, c, more):
                        if c < NC - 1:
                            scan_inputs(i, p, c + 1)
                        elif more:
                            scan_inputs(i + 1, 1 - p, 0)
                        if c < HC:
                            aneg_of[0] = aneg[p]
                            if c == 0 and not is0(i):
                                act.wait_ge(s_scan, i * UN)
                            decays(i, 1, c)

                    bodies(act, prepare, chunk, lambda i, p: None, open_=lambda: scan_inputs(0, 0, 0))

                @block.gpsimd
                def _(pool):
                    pool.memset(zeros[:, :], 0.0).then_inc(s_init, 1)
                    for et in range(ET):
                        pool.memset(cv[et][:, 0:KC - 1], 0.0).then_inc(s_init, 1)
                    pool.wait_ge(s_c, 16 * 5)

                    def kernel_of(i, p, c):
                        if c == 0:
                            pool.wait_ge(s_xpc, i * 3 + 3)
                        if not (is0(i) and c < 2):
                            pool.wait_ge(s_v, (i * NC + c - 1) * ET)
                        if c > 1:
                            pool.wait_ge(s_ca, i * (NC - 1) + c - 1)
                        elif c == 0 and not is0(i):
                            pool.wait_ge(s_ca, i * (NC - 1))
                        pool.tensor_tensor(g[c % 2][0:CH, :, :], kern[:, :].unsqueeze(1).broadcast_to([CH, NS, CH]),
                                           bt[p][:, c, :].unsqueeze(2).broadcast_to([CH, NS, CH]), ALU.mult).then_inc(s_g, 1)

                    def first_decays(i, half):
                        pool.wait_ge(s_da, i * 8 + half * 4 + 4)
                        pool.sem_inc(s_passed["pool"], 1)
                        d0 = decay[:, half, :, :, :, 0].rearrange("p e c n -> p (e c n)")
                        pool.tensor_copy(decay0[:, half, :, :, :].rearrange("p e c n -> p (e c n)"), d0).then_inc(s_d0c, 1)
                        pool.wait_ge(s_d0c, i * 2 + half + 1)
                        pool.sem_inc(s_passed["pool"], 1)
                        pool.memset(d0, 0.0).then_inc(s_d0, 1)

                    def prepare(i, p, c):
                        if c == NC - 1:
                            first_decays(i, 0)

                    def times_c(i, p, c, et):
                        k = (c % 2) * ET + et
                        if et == 0:
                            pool.wait_ge(s_cb[c], i * 16 + 16)
                        pool.wait_ge(s_scan, (i * NC + c) * ET + et + 1)
                        if not (is0(i) and c < 2):
                            pool.wait_ge(s_y, (i * NC + c - 2) * ET + et + 1)
                        pool.tensor_tensor(hc[k][:, :, :], h[et][:, :, :], cb[:, c, :, :], ALU.mult).then_inc(s_hc, 1)

                    def chunk(i, p, c, more):
                        if c < NC - 1:
                            kernel_of(i, p, c + 1)
                        elif more:
                            kernel_of(i + 1, 1 - p, 0)
                        for et in range(ET):
                            times_c(i, p, c, et)
                        if c == HC - 1:
                            first_decays(i, 1)

                    bodies(pool, prepare, chunk, lambda i, p: None, open_=lambda: kernel_of(0, 0, 0))

                @block.vector
                def _(dve):
                    dve.memset(eps[:, :], EPS).then_inc(s_eps, 1)
                    for c in range(NB):
                        dve.wait_ge(s_mean, c + 1)
                        dve.tensor_tensor(ln_x(c), x[:, c, :], ps[:, c, :], ALU.subtract).then_inc(s_lnx, 1)
                    for c in range(NB):
                        dve.wait_ge(s_lnx, c + 1)
                        dve.wait_ge(s_lnrs, c + 1)
                        dve.tensor_tensor(a[:, c, :], ln_x(c), ln_rs(c), ALU.mult).then_inc(s_a, 1)

                    def prepare(i, p, c):
                        if c == 0:
                            dve.wait_ge(s_rs, i + 1)
                            dve.wait_ge(s_wt[p], (i // 2) * 16 + 16 if isinstance(i, int) else (i >> 1) * 16 + 16)
                            dve.scalar_tensor_tensor(xr[:, :].unsqueeze(1), a[:, bass.ds(i & (NB - 1), 1), :], w(p, "norm_w"),
                                                     rs[:, :].unsqueeze(1), ALU.mult, ALU.mult).then_inc(s_xr, 1)
                        if c == 1:
                            for et, bank in ((0, bank_a), (1, bank_b)):
                                dve.wait_ge(s_szs, i * ET + et + 1)
                                dve.tensor_tensor(sz[p][:, et, :], bank, sig[:, :], ALU.mult).then_inc(s_sz, 1)
                            dve.wait_ge(s_al, i + 1)
                            dve.tensor_scalar(aneg[p][:, :], aexp[:, :], -1.0, None, ALU.mult).then_inc(s_an, 1)
                        if c == 2:
                            for et in range(ET):
                                dve.wait_ge(s_cv, i * ET + et + 1)
                                if et:
                                    dve.wait_ge(s_xb, i * ET + et)
                                elif not is0(i):
                                    dve.wait_ge(s_delta, i * ET)
                                dve.tensor_scalar(conv[:, :], cv[et][:, 0:L], w(p, "conv_w", et * KC), w(p, "conv_b", et),
                                                  ALU.mult, ALU.add).then_inc(s_cd, 1)
                                for k in range(1, KC):
                                    dve.wait_ge(s_cd, (i * ET + et) * KC + k)
                                    dve.scalar_tensor_tensor(conv[:, :], cv[et][:, k:k + L], w(p, "conv_w", et * KC + k), conv[:, :],
                                                             ALU.mult, ALU.add).then_inc(s_cd, 1)
                                dve.wait_ge(s_cs, i * ET + et + 1)
                                dve.tensor_tensor(xb[p][:, et, :], conv[:, :], sig[:, :], ALU.mult).then_inc(s_xb, 1)
                        if c == 3:
                            for et, bank in ((0, bank_a), (1, bank_b)):
                                n = (i * ET + et) * 6
                                dve.wait_ge(s_ex, i * ET + et + 1)
                                dve.tensor_scalar(sig[:, :], ex[:, :], SMALL, None, ALU.is_lt).then_inc(s_sd, 1)
                                dve.tensor_scalar(mag[:, :], ex[:, :], -1.0 / 4, 1.0 / 3, ALU.mult, ALU.add).then_inc(s_sd, 1)
                                dve.wait_ge(s_sd, n + 2)
                                dve.tensor_tensor(mag[:, :], mag[:, :], ex[:, :], ALU.mult).then_inc(s_sd, 1)
                                dve.wait_ge(s_sd, n + 3)
                                dve.scalar_tensor_tensor(mag[:, :], mag[:, :], -0.5, ex[:, :], ALU.add, ALU.mult).then_inc(s_sd, 1)
                                dve.wait_ge(s_sd, n + 4)
                                dve.scalar_tensor_tensor(mag[:, :], mag[:, :], 1.0, ex[:, :], ALU.add, ALU.mult).then_inc(s_sd, 1)
                                dve.wait_ge(s_sd, n + 5)
                                dve.wait_ge(s_sp, (i * ET + et) * 2 + 1)
                                dve.sem_inc(s_passed["dve"], 1)
                                dve.copy_predicated(lg[:, :], sig[:, :].bitcast(mybir.dt.uint32), mag[:, :]).then_inc(s_sd, 1)
                                dve.wait_ge(s_sd, n + 6)
                                dve.wait_ge(s_sp, (i * ET + et) * 2 + 2)
                                if et == 0 and not is0(i):
                                    dve.wait_ge(s_da, i * 8)
                                dve.tensor_tensor(delta[:, et, :], lin[:, :], lg[:, :], ALU.add).then_inc(s_delta, 1)
                                dve.wait_ge(s_delta, i * ET + et + 1)
                                dve.tensor_tensor(u[p][:, et, :], delta[:, et, :], xb[p][:, et, :], ALU.mult).then_inc(s_u, 1)

                    def reduce_states(i, c, et):
                        dve.wait_ge(s_hc, (i * NC + c) * ET + et + 1)
                        dve.tensor_reduce(y[:, et, c * CH:(c + 1) * CH], hc[(c % 2) * ET + et][:, :, :].rearrange("p n t -> p t n"),
                                          AX.X, ALU.add).then_inc(s_y, 1)

                    def chunk(i, p, c, more):
                        for et in range(ET):
                            un = (i * NC + c) * ET + et
                            half, ch = c // HC, c % HC
                            if c % HC == 0 and et == 0:
                                dve.wait_ge(s_d0, i * 2 + half + 1)
                            if c:
                                t = i * (NC - 1) * ET * 2 + ((c - 1) * ET + et) * 2
                                dve.wait_ge(s_scan, un - 1)
                                dve.tensor_tensor(carry_in[:, :], decay0[:, half, et, ch, :], h[et][:, :, CH - 1], ALU.mult).then_inc(s_t0, 1)
                                reduce_states(i, c - 1, et)
                                dve.wait_ge(s_t0, t + 1)
                                dve.wait_ge(s_v, un + 1)
                                dve.tensor_tensor(ps_v[et][:, :, 0], ps_v[et][:, :, 0], carry_in[:, :], ALU.add).then_inc(s_t0, 1)
                                dve.wait_ge(s_t0, t + 2)
                            dve.wait_ge(s_v, un + 1)
                            if not (is0(i) and c == 0):
                                dve.wait_ge(s_hc, un - 1)
                            dve.tensor_tensor_scan(h[et][:, :, :].rearrange("p n t -> p (n t)"),
                                                   decay[:, half, et, ch, :, :].rearrange("p n t -> p (n t)"),
                                                   ps_v[et].rearrange("p n t -> p (n t)"), 0.0, ALU.mult, ALU.add).then_inc(s_scan, 1)

                    def finish(i, p):
                        for et in range(ET):
                            reduce_states(i, NC - 1, et)
                        for et in range(ET):
                            dve.wait_ge(s_y, (i * NC + NC - 1) * ET + et + 1)
                            dve.scalar_tensor_tensor(y[:, et, :], xb[p][:, et, :], w(p, "dp", et), y[:, et, :], ALU.mult, ALU.add)\
                               .then_inc(s_yd, 1)
                            dve.wait_ge(s_yd, i * ET + et + 1)
                            dve.tensor_tensor(y[:, et, :], y[:, et, :], sz[p][:, et, :], ALU.mult).then_inc(s_yg, 1)
                        dve.wait_ge(s_op, i + 1)
                        at = bass.ds(i & (NB - 1), 1)
                        dve.tensor_tensor(a[:, at, :], a[:, at, :], bank_c.unsqueeze(1), ALU.add).then_inc(s_res, 1)

                    bodies(dve, prepare, chunk, finish)
                    dve.wait_ge(s_res, NL * NB)
                    dve.tensor_tensor(x[:, :, :], x[:, :, :], a[:, :, :], ALU.add).then_inc(s_end, 1)
                    dve.wait_ge(s_end, 1)


def macaron(nc, dram):
    with ExitStack() as ctx:
        x = ctx.enter_context(nc.sbuf_tensor("x_res", [D, NB, L], F32))
        Ffn(nc, x, dram["x"], None, dram, None, "f1").build()
        Mamba(nc, x, dram).build()
        Ffn(nc, x, None, dram["out"], dram, None, "f2").build()


def kernel(**inputs):
    import concourse.bacc as _bacc
    from concourse.bass_utils import run_bass_kernel_spmd as _run

    f = {k.replace("L0_attn_", "m_").replace("L0_ffn_", "f_"): np.asarray(v) for k, v in inputs.items()}
    lay = np.ascontiguousarray
    arrays = {
        "x": lay(f["m_x"].reshape(NB, L, D).transpose(2, 0, 1)),
        "w1": lay(f["f_W1"].reshape(E, D, FT, 128).transpose(1, 0, 2, 3).reshape(D, S1, 128)),
        "w2": lay(f["f_W2"].reshape(E, FT, 128, D).transpose(2, 0, 1, 3).reshape(128, S1, D)),
        "b1": lay(f["f_b1"].reshape(S1, 128).T),
        "b2": lay(f["f_b2"].T),
        "wr": lay(f["f_Wr"]),
        "br": lay(np.broadcast_to(f["f_br"][None, :], (128, E))),
    }
    def tiles(v):
        return v.reshape(NL, ET, 128, -1).transpose(0, 2, 1, 3).reshape(NL, 128, -1)

    dt_w = np.zeros((NL, 128, EI), np.float32)
    dt_w[:, :R, :] = f["m_dt_w"].transpose(0, 2, 1)
    parts = {
        "in_w": f["m_in_proj_w"].transpose(0, 2, 1),
        "xp": tiles(f["m_x_proj_w"].transpose(0, 2, 1)),
        "out_w": tiles(f["m_out_w"].transpose(0, 2, 1)),
        "conv_w": tiles(f["m_conv_w"]),
        "conv_b": tiles(f["m_conv_b"]),
        "dt_b": tiles(f["m_dt_b"]),
        "a_log": tiles(f["m_A_log"]),
        "dp": tiles(f["m_Dp"]),
        "norm_w": f["m_norm_w"].reshape(NL, D, 1),
        "dt_w": dt_w,
    }
    arrays["mw"] = lay(np.concatenate([parts[n] for n, _ in PACK], axis=2))
    t = np.arange(CH)
    arrays["ones"] = np.full((128, 128), 1.0 / D, np.float32)
    arrays["ident"] = np.eye(128, dtype=np.float32)
    arrays["sel"] = lay(np.broadcast_to(np.eye(E, dtype=np.float32)[:, :, None], (E, E, 128)))
    lag = t[None, :] - t[:, None]
    arrays["kern"] = np.where(lag >= 0, BETA ** np.maximum(lag, 0).astype(np.float64), 0.0).astype(np.float32)
    arrays["carry_kern"] = (np.eye(NS)[:, :, None] * BETA ** (t + 1.0)[None, None, :]).astype(np.float32)

    nc = _bacc.Bacc("TRN2", target_bir_lowering=False, num_devices=1)
    dram = {n: nc.dram_tensor(f"in_{n}", v.shape, F32, kind="ExternalInput").ap() for n, v in arrays.items()}
    dram["out"] = nc.dram_tensor("out_x", (D, NB, L), F32, kind="ExternalOutput").ap()
    dram["c_scratch"] = nc.dram_tensor("c_scratch", (NC, NS, CH), F32, kind="Internal").ap()
    macaron(nc, dram)
    r = _run(nc, [{f"in_{n}": v for n, v in arrays.items()}], core_ids=[0])
    return lay(np.asarray(r.results[0]["out_x"]).transpose(1, 2, 0))
```

```python
from contextlib import ExitStack

import concourse.bass as bass
import numpy as np
from concourse import mybir

F32 = mybir.dt.float32
ALU = mybir.AluOpType
ACT = mybir.ActivationFunctionType
AX = mybir.AxisListType
TABLES = "natural_log_exp_and_others"

D = 128
NB = 4
L = 512
E = 8
F = 512
FT = F // 128
S1 = E * FT
TT = L // 128
EI = 256
ET = EI // 128
NS = 16
R = 8
KC = 4
NL = 2
CH = 64
NC = L // CH
UN = NC * ET
CW = NS * CH
HC = NC // 2
BETA = 0.6
EPS = 1e-5
ITERS = 25
SMALL = 1.0 / 32

XW = 32 + 2 * NS
PACK_IN = [("in_w", 2 * EI), ("xp", ET * XW), ("conv_w", ET * KC), ("conv_b", ET), ("dt_b", ET),
           ("a_log", ET * NS), ("norm_w", 1), ("dt_w", EI)]
PACK_OUT = [("out_w", ET * D), ("dp", ET)]


def columns(pack):
    at, col = 0, {}
    for name, n in pack:
        col[name] = at
        at += n
    return col, at


COL_IN, NW_IN = columns(PACK_IN)
COL_OUT, NW_OUT = columns(PACK_OUT)


class Ffn:

    def __init__(self, nc, x, src, out, dram, consts, tag):
        self.nc, self.x, self.src, self.out, self.dram, self.tag = nc, x, src, out, dram, tag
        self.consts = consts

    def build(self):
        nc, x, tag = self.nc, self.x, self.tag
        with ExitStack() as ctx:
            def sb(name, shape):
                return ctx.enter_context(nc.sbuf_tensor(f"{name}_{tag}", shape, F32))

            def sem(name):
                return ctx.enter_context(nc.semaphore(f"{name}_{tag}"))

            ps = ctx.enter_context(nc.psum_tensor(f"ps_{tag}", [128, 8, 512], F32))
            ps_hidden = [ps[:, 0, :], ps[:, 1, :]]
            ps_y = [ps[:, 2, :], ps[:, 3, :]]
            ps_gate = ps[:, 4, :]
            ps_logit = ps[:, 7, 0:NB * TT * E]
            ps_gT = ps[0:E, 5, :]

            w1 = sb("w1", [D, S1, 128])
            w2 = sb("w2", [128, S1, D])
            b1 = sb("b1", [128, S1])
            b2 = sb("b2", [D, E])
            wr = sb("wr", [D, E])
            br = sb("br", [128, E])
            ones = sb("ones", [128, 128])
            ident = sb("ident", [128, 128])
            sel = sb("sel", [E, E, 128])
            eps = sb("eps", [128, 1])
            xn = sb("xn", [D, NB, L])
            hidden = sb("hidden", [128, 4, L])
            yb = sb("yb", [D, E, L])
            prod = sb("prod", [D, L])
            acc = sb("acc", [D, L])
            G = NB * TT
            xs = sb("xs", [128, G, E])
            z = sb("z", [128, G, E])
            z2 = sb("z2", [128, G, E])
            gates = sb("gates", [128, G, E])
            mask = sb("mask", [128, G, E])
            mx = sb("mx", [128, G])
            lo = sb("lo", [128, G])
            dm = sb("dm", [128, G])
            tau = sb("tau", [128, G])
            f_lo = sb("f_lo", [128, G])
            f_m = sb("f_m", [128, G])
            step = sb("step", [128, G])
            gT = sb("gT", [E, NB * L])

            s_x = sem("x_loaded")
            s_c = sem("constants_loaded")
            s_w1 = [sem(f"w1_{e}_loaded") for e in range(E)]
            s_w2 = [sem(f"w2_{e}_loaded") for e in range(E)]
            s_mean = sem("mean_ready")
            s_xc = sem("centred_ready")
            s_sq = sem("squares_ready")
            s_var = sem("variance_ready")
            s_lnv = sem("log_variance_ready")
            s_rs = sem("rstd_ready")
            s_xn = sem("normed_ready")
            s_log = sem("logits_ready")
            s_dve = sem("gating_step_done")
            s_exp = sem("gating_log_done")
            s_gates = sem("gates_ready")
            s_gt = sem("gates_transposed")
            s_gtc = sem("gates_copied")
            s_gb = sem("gate_broadcast")
            s_mm1 = sem("hidden_product_ready")
            s_h = sem("hidden_ready")
            s_mm2 = sem("hidden_used")
            s_y = sem("expert_output_ready")
            s_prod = sem("gated_output_ready")
            s_acc = sem("gated_sum_ready")
            s_new = sem("x_updated")
            s_out = sem("x_stored")
            s_passed = sem("wait_passed")
            LAG = 2

            with nc.Block() as block:
                @block.sync
                def _(sp):
                    if self.src is not None:
                        sp.dma_start(x[:, :, :], self.src).then_inc(s_x, 16)
                    for t, name in ((b1, "b1"), (b2, "b2"), (wr, "wr"), (ones, "ones"), (ident, "ident"), (sel, "sel"), (br, "br")):
                        src = self.dram[name]
                        sp.dma_start(t[tuple([slice(None)] * len(t.shape))], src).then_inc(s_c, 16)
                    for e in range(E):
                        sp.dma_start(w1[:, e * FT:(e + 1) * FT, :], self.dram["w1"][:, e * FT:(e + 1) * FT, :]).then_inc(s_w1[e], 16)
                        sp.dma_start(w2[:, e * FT:(e + 1) * FT, :], self.dram["w2"][:, e * FT:(e + 1) * FT, :]).then_inc(s_w2[e], 16)
                    if self.out is not None:
                        for c in range(NB):
                            sp.wait_ge(s_new, c + 1)
                            sp.dma_start(self.out[:, c, :], x[:, c, :]).then_inc(s_out, 16)
                        sp.wait_ge(s_out, 16 * NB)

                @block.tensor
                def _(pe):
                    if self.src is not None:
                        pe.wait_ge(s_x, 16)
                    pe.wait_ge(s_c, 16 * 7)
                    for c in range(NB):
                        pe.matmul(ps[:, c, :], ones[:, :], x[:, c, :], start=True, stop=True).then_inc(s_mean, 1)
                    for c in range(NB):
                        pe.wait_ge(s_sq, c + 1)
                        pe.matmul(ps[:, NB + c, :], ones[:, :], hidden[:, c, :], start=True, stop=True).then_inc(s_var, 1)
                    pe.wait_ge(s_xn, NB)
                    for t in range(NB * TT):
                        mm = pe.matmul(ps_logit[:, t * E:(t + 1) * E], xn[:, t // TT, (t % TT) * 128:(t % TT + 1) * 128], wr[:, :],
                                       start=True, stop=True)
                    mm.then_inc(s_log, 1)

                    def hidden_product(c, s):
                        if isinstance(c, int) and c == 0 and s % FT == 0:
                            pe.wait_ge(s_w1[s // FT], 16)
                        if not (isinstance(c, int) and c == 0 and s < 2):
                            pe.wait_ge(s_h, c * S1 + s - 1)
                        pe.matmul(ps_hidden[s % 2], w1[:, s, :], xn[:, bass.ds(c, 1), :], start=True, stop=True).then_inc(s_mm1, 1)

                    def expert_product(c, s):
                        e, f = s // FT, s % FT
                        if isinstance(c, int) and c == 0 and f == 0:
                            pe.wait_ge(s_w2[e], 16)
                        if f == 0 and not (isinstance(c, int) and c == 0 and e < 2):
                            pe.wait_ge(s_y, c * E + e - 1)
                        pe.wait_ge(s_h, c * S1 + s + 1)
                        mm = pe.matmul(ps_y[e % 2], w2[:, s, :], hidden[:, s % 4, :], start=(f == 0), stop=(f == FT - 1))
                        mm.then_inc(s_mm2, 1)

                    def gate_broadcast(c, e):
                        pe.wait_ge(s_prod, c * E + e + 1)
                        pe.sem_inc(s_passed, 1)
                        pe.matmul(ps_gate, sel[:, e, :], gT[:, bass.ds(c * L, L)], start=True, stop=True).then_inc(s_gb, 1)

                    def batch(c, gates_of):
                        for s in range(S1 + LAG):
                            if s < S1:
                                if gates_of is not None and s % FT == 0:
                                    gate_broadcast(gates_of, s // FT)
                                hidden_product(c, s)
                            if s >= LAG:
                                expert_product(c, s - LAG)

                    batch(0, None)
                    pe.wait_ge(s_gates, 1)
                    for c in range(NB):
                        if c:
                            pe.wait_ge(s_gtc, c)
                        for t in range(TT):
                            mm = pe.transpose(ps_gT[:, t * 128:(t + 1) * 128], gates[:, c * TT + t, :], ident[:, :])
                        mm.then_inc(s_gt, 1)
                    pe.wait_ge(s_gtc, NB)
                    with pe.Fori(1, NB) as c:
                        batch(c, c - 1)
                    for e in range(E):
                        gate_broadcast(NB - 1, e)

                @block.scalar
                def _(act):
                    act.preload_act_table_set(TABLES)
                    act.wait_ge(s_c, 16 * 7)
                    for c in range(NB):
                        act.wait_ge(s_xc, c + 1)
                        act.activation(hidden[:, c, :], yb[:, c, :], ACT.Square).then_inc(s_sq, 1)
                    for c in range(NB):
                        act.wait_ge(s_var, c + 1)
                        act.activation(yb[:, NB + c, :], ps[:, NB + c, :], ACT.Ln, bias=eps[:, 0:1]).then_inc(s_lnv, 1)
                    for c in range(NB):
                        act.wait_ge(s_lnv, c + 1)
                        act.activation(yb[:, NB + c, :], yb[:, NB + c, :], ACT.Exp, scale=-0.5).then_inc(s_rs, 1)

                    def relu(c, s):
                        act.wait_ge(s_mm1, c * S1 + s + 1)
                        if not (isinstance(c, int) and c == 0 and s < 4):
                            act.wait_ge(s_mm2, c * S1 + s - 3)
                        act.activation(hidden[:, s % 4, :], ps_hidden[s % 2], ACT.Relu, bias=b1[:, s:s + 1]).then_inc(s_h, 1)

                    def expert_out(c, e):
                        act.wait_ge(s_mm2, c * S1 + (e + 1) * FT)
                        if not (isinstance(c, int) and c == 0):
                            act.wait_ge(s_prod, (c - 1) * E + e + 2)
                        act.activation(yb[:, e, :], ps_y[e % 2], ACT.Identity, bias=b2[:, e:e + 1]).then_inc(s_y, 1)

                    def batch(c):
                        for s in range(S1 + LAG + 1):
                            if s < S1:
                                relu(c, s)
                            if s > LAG and (s - LAG - 1) % FT == FT - 1:
                                expert_out(c, (s - LAG - 1) // FT)

                    batch(0)
                    with act.Fori(1, NB) as c:
                        batch(c)

                @block.vector
                def _(dve):
                    dve.sem_inc(s_prod, 1)
                    dve.memset(eps[:, :], EPS).then_inc(s_dve, 1)
                    for c in range(NB):
                        dve.wait_ge(s_mean, c + 1)
                        dve.tensor_tensor(yb[:, c, :], x[:, c, :], ps[:, c, :], ALU.subtract).then_inc(s_xc, 1)
                    for c in range(NB):
                        dve.wait_ge(s_xc, c + 1)
                        dve.wait_ge(s_rs, c + 1)
                        dve.tensor_tensor(xn[:, c, :], yb[:, c, :], yb[:, NB + c, :], ALU.mult).then_inc(s_xn, 1)

                    done = [1]

                    def then(ins):
                        done[0] += 1
                        ins.then_inc(s_dve, 1)
                        dve.wait_ge(s_dve, done[0])

                    def wide(t):
                        return t[:, :].unsqueeze(2).broadcast_to([128, G, E])

                    def power_sum(out, tau_ap):
                        then(dve.tensor_tensor(z[:, :, :], xs[:, :, :], tau_ap, ALU.subtract))
                        then(dve.scalar_tensor_tensor(z2[:, :, :], z[:, :, :], 0.0, z[:, :, :], ALU.max, ALU.mult))
                        then(dve.tensor_reduce(out[:, :], z2[:, :, :], AX.X, ALU.add))

                    dve.wait_ge(s_log, 1)
                    dve.wait_ge(s_c, 16 * 7)
                    lg = ps_logit.rearrange("p (g e) -> p g e", e=E)
                    then(dve.tensor_tensor(z[:, :, :], lg, br[:, :].unsqueeze(1).broadcast_to([128, G, E]), ALU.add))
                    then(dve.tensor_scalar(xs[:, :, :], z[:, :, :], 0.5, None, ALU.mult))
                    then(dve.tensor_reduce(mx[:, :], xs[:, :, :], AX.X, ALU.max))
                    then(dve.tensor_scalar(lo[:, :], mx[:, :], -1.0, None, ALU.add))
                    then(dve.tensor_scalar(dm[:, :], mx[:, :], -float(np.float32((1.0 / E) ** 0.5)), None, ALU.add))
                    then(dve.tensor_tensor(dm[:, :], dm[:, :], lo[:, :], ALU.subtract))
                    power_sum(f_lo, wide(lo))
                    then(dve.tensor_scalar(f_lo[:, :], f_lo[:, :], -1.0, None, ALU.add))
                    for k in range(ITERS):
                        half = 0.5 ** (k + 1)
                        then(dve.scalar_tensor_tensor(tau[:, :], dm[:, :], half, lo[:, :], ALU.mult, ALU.add))
                        power_sum(f_m, wide(tau))
                        if k < ITERS - 1:
                            then(dve.scalar_tensor_tensor(step[:, :], f_m[:, :], -1.0, f_lo[:, :], ALU.add, ALU.mult))
                            then(dve.scalar_tensor_tensor(step[:, :], step[:, :], 0.0, dm[:, :], ALU.is_ge, ALU.mult))
                            then(dve.scalar_tensor_tensor(lo[:, :], step[:, :], half, lo[:, :], ALU.mult, ALU.add))
                    then(dve.reciprocal(step[:, :], f_m[:, :]))
                    then(dve.tensor_tensor(z[:, :, :], z2[:, :, :], wide(step), ALU.mult))
                    dve.scalar_tensor_tensor(gates[:, :, :], z[:, :, :], 1e-9, z[:, :, :], ALU.is_gt, ALU.mult).then_inc(s_gates, 1)
                    for c in range(NB):
                        dve.wait_ge(s_gt, c + 1)
                        dve.tensor_copy(gT[:, c * L:(c + 1) * L], ps_gT).then_inc(s_gtc, 1)

                    def combine(c):
                        for e in range(E):
                            dve.wait_ge(s_gb, c * E + e + 1)
                            dve.wait_ge(s_y, c * E + e + 1)
                            if e == 0:
                                if not isinstance(c, int):
                                    dve.wait_ge(s_new, c)
                                dve.tensor_tensor(acc[:, :], yb[:, e, :], ps_gate, ALU.mult).then_inc(s_prod, 1)
                                continue
                            if e > 1:
                                dve.wait_ge(s_acc, c * (E - 1) + e - 1)
                            dve.tensor_tensor(prod[:, :], yb[:, e, :], ps_gate, ALU.mult).then_inc(s_prod, 1)
                            dve.wait_ge(s_prod, c * E + e + 2)
                            dve.tensor_tensor(acc[:, :], acc[:, :], prod[:, :], ALU.add).then_inc(s_acc, 1)
                        dve.wait_ge(s_acc, (c + 1) * (E - 1))
                        dve.scalar_tensor_tensor(x[:, bass.ds(c, 1), :], acc[:, :].unsqueeze(1), 0.5, x[:, bass.ds(c, 1), :], ALU.mult, ALU.add)\
                           .then_inc(s_new, 1)

                    combine(0)
                    with dve.Fori(1, NB) as c:
                        combine(c)


class Mamba:

    def __init__(self, nc, x, dram):
        self.nc, self.x, self.dram = nc, x, dram

    def build(self):
        nc, x, dram = self.nc, self.x, self.dram
        PAIRS = NL * NB
        with ExitStack() as ctx:
            def sb(name, shape):
                return ctx.enter_context(nc.sbuf_tensor(name, shape, F32))

            def sem(name):
                return ctx.enter_context(nc.semaphore(name))

            ps = ctx.enter_context(nc.psum_tensor("ps_m", [128, 8, 512], F32))
            ps_v = [ps[:, 2 * et:2 * et + 2, :].rearrange("p b (n t) -> p (b n) t", t=CH) for et in range(ET)]
            ps_v_half = [[ps[:, 2 * et + b, :] for b in range(2)] for et in range(ET)]
            ps_uT = ps[0:CH, 4, 0:EI]
            ps_carry = ps[0:NS, 4, EI:2 * EI]
            bank_a, bank_b, bank_c = ps[:, 5, :], ps[:, 6, :], ps[:, 7, :]
            bank_of = (bank_b, bank_c)

            a = sb("a", [D, NB, L])
            w_in = sb("w_in", [128, NW_IN])
            w_out = [sb(f"w_out{p}", [128, NW_OUT]) for p in range(2)]
            ones = sb("ones_m", [128, 128])
            ident = sb("ident_m", [128, 128])
            kern = sb("kern", [CH, CH])
            eps = sb("eps_m", [128, 1])
            decay = sb("decay", [128, 2, ET, HC, NS, CH])
            decay0 = sb("decay0", [128, 2, ET, HC, NS])
            cb = sb("cb", [128, NC, NS, CH])
            g = [sb(f"g{p}", [CH + NS, NS, CH]) for p in range(2)]
            su = [sb(f"su{p}", [CH + NS, EI]) for p in range(2)]
            h = [sb(f"h{et}", [128, NS, CH]) for et in range(ET)]
            hc = [sb(f"hc{k}", [128, NS, CH]) for k in range(4)]
            carry_in = sb("carry_in", [128, NS])
            sq = sb("sq_m", [D, L])
            rs = sb("rs_m", [D, L])
            xr = sb("xr", [D, L])
            cv = [sb(f"cv{et}", [128, KC - 1 + L]) for et in range(ET)]
            conv = [sb(f"conv{et}", [128, L]) for et in range(ET)]
            sig = [sb(f"sig{et}", [128, L]) for et in range(ET)]
            xb = [sb(f"xb{p}", [128, ET, L]) for p in range(2)]
            sz = [sb(f"sz{p}", [128, ET, L]) for p in range(2)]
            u = [sb(f"u{p}", [128, ET, L]) for p in range(2)]
            bt = [sb(f"bt{p}", [CH, NC, NS]) for p in range(2)]
            dtc = sb("dtc", [CH + NS, L])
            dtr, csb, zeros = dtc[0:R, :], dtc[32:32 + NS, :], dtc[CH:CH + NS, 0:EI]
            mag, ex, lg, lin = sq, rs, xr, conv
            delta = sb("delta", [128, ET, L])
            aexp = sb("aexp", [128, ET * NS])
            aneg = [sb(f"aneg{p}", [128, ET * NS]) for p in range(2)]
            y = sb("y", [128, ET, L])
            ln_x, ln_sq, ln_rs = (lambda c, t=t: t[c // ET][:, c % ET, :] for t in (u, sz, xb))

            s_c = sem("m_constants_loaded")
            s_init = sem("m_fills_done")
            s_eps = sem("m_eps_filled")
            s_wi = sem("m_in_weights_loaded")
            s_wo = [sem(f"m_out_weights{p}_loaded") for p in range(2)]
            s_mean = sem("m_mean_ready")
            s_lnx = sem("m_centred_ready")
            s_lnsq = sem("m_ln_squares_ready")
            s_lnvar = sem("m_ln_variance_ready")
            s_lnlog = sem("m_ln_log_ready")
            s_lnrs = sem("m_ln_rstd_ready")
            s_a = sem("m_layernorm_ready")
            s_sq = sem("m_squares_ready")
            s_ms = sem("m_mean_square_ready")
            s_log = sem("m_log_ready")
            s_rs = sem("m_rstd_ready")
            s_xr = sem("m_normed_ready")
            s_xi = sem("m_inner_product_ready")
            s_cv = sem("m_inner_copied")
            s_z = sem("m_gate_product_ready")
            s_zc = sem("m_gate_copied")
            s_zs = sem("m_gate_sigmoid_step")
            s_zsig = sem("m_gate_sigmoid_ready")
            s_sz = sem("m_gate_silu_ready")
            s_cd = sem("m_conv_step")
            s_cst = sem("m_conv_sigmoid_step")
            s_cs = sem("m_conv_sigmoid_ready")
            s_xb = sem("m_inner_silu_ready")
            s_xp = sem("m_x_products_ready")
            s_xpc = sem("m_x_products_copied")
            s_dtp = sem("m_dt_product_ready")
            s_mag = sem("m_dt_magnitude_ready")
            s_ex = sem("m_dt_exp_ready")
            s_sp = sem("m_dt_log_and_relu_ready")
            s_sd = sem("m_softplus_step")
            s_delta = sem("m_delta_ready")
            s_u = sem("m_u_ready")
            s_al = sem("m_a_exp_ready")
            s_an = sem("m_a_ready")
            s_da = sem("m_decay_ready")
            s_d0 = sem("m_decay0_ready")
            s_d0c = sem("m_decay0_copied")
            s_cs_st = sem("m_c_stored")
            s_cb = [sem(f"m_c{c}_spread") for c in range(NC)]
            s_g = sem("m_kernel_ready")
            s_uT = sem("m_uT_ready")
            s_ca = sem("m_carry_product_ready")
            s_su = sem("m_scan_inputs_ready")
            s_v = sem("m_v_ready")
            s_t0 = sem("m_carry_step")
            s_scan = sem("m_scan_done")
            s_hc = sem("m_hc_ready")
            s_y = sem("m_y_reduced")
            s_yd = sem("m_y_skip_added")
            s_yg = sem("m_y_gated")
            s_op = sem("m_out_product_ready")
            s_res = sem("m_residual_added")
            s_end = sem("m_x_updated")
            s_passed = {name: sem(f"m_wait_passed_{name}") for name in ("pe", "pool", "sp", "dve")}

            def wi(name, k=0, n=1, rows=128):
                at = COL_IN[name] + k
                return w_in[0:rows, at:at + n]

            def wo(p, name, k=0, n=1):
                at = COL_OUT[name] + k
                return w_out[p][:, at:at + n]

            def is0(i):
                return isinstance(i, int) and i == 0

            def pairs(eng, prologue, slot, epilogue):
                def body(i, p, prev, more):
                    for c in range(NC):
                        for et in range(ET):
                            slot(i, p, c, et, prev, more)

                prologue()
                body(0, 0, False, True)
                with eng.Fori(0, PAIRS // 2 - 1) as j:
                    body(j * 2 + 1, 1, True, True)
                    body(j * 2 + 2, 0, True, True)
                body(PAIRS - 1, 1, True, False)
                epilogue()

            with nc.Block() as block:
                @block.sync
                def _(sp):
                    for t, name in ((ones, "ones"), (ident, "ident"), (kern, "kern")):
                        sp.dma_start(t[:, :], dram[name]).then_inc(s_c, 16)
                    for p in range(2):
                        sp.dma_start(g[p][CH:CH + NS, :, :], dram["carry_kern"]).then_inc(s_c, 16)

                    def layer_of(t, i):
                        layer = (i // NB) & (NL - 1)
                        if isinstance(layer, int):
                            return dram[t][layer, :, :]
                        return dram[t][bass.ds(layer, 1), :, :].rearrange("o p n -> (o p) n")

                    def load_in(i):
                        if not is0(i):
                            sp.wait_ge(s_sp, i * ET * 2)
                            sp.sem_inc(s_passed["sp"], 1)
                        sp.dma_start(w_in[:, :], layer_of("w_in", i)).then_inc(s_wi, 16)

                    def load_out(i, p):
                        if not (isinstance(i, int) and i < 2):
                            sp.wait_ge(s_res, i - 1)
                            sp.sem_inc(s_passed["sp"], 1)
                        sp.dma_start(w_out[p][:, :], layer_of("w_out", i)).then_inc(s_wo[p], 16)

                    def store_c(i):
                        sp.wait_ge(s_xpc, i * 3 + 2)
                        sp.sem_inc(s_passed["sp"], 1)
                        if not is0(i):
                            for k in range(NC):
                                sp.wait_ge(s_cb[k], i * 16)
                        sp.dma_start(dram["c_scratch"].rearrange("c n t -> n c t"),
                                     csb.rearrange("n (c t) -> n c t", t=CH)).then_inc(s_cs_st, 16)
                        sp.wait_ge(s_cs_st, i * 16 + 16)
                        sp.sem_inc(s_passed["sp"], 1)

                    def spread_c(i, k):
                        if not is0(i):
                            sp.wait_ge(s_hc, (i - 1) * UN + ET * (k + 1))
                        sp.dma_start(cb[:, k, :, :], dram["c_scratch"][k:k + 1, :, :].broadcast_to([128, NS, CH]))\
                          .then_inc(s_cb[k], 16)

                    def prologue():
                        load_in(0)
                        load_out(0, 0)
                        store_c(0)
                        load_in(1)
                        for k in range(NC):
                            spread_c(0, k)

                    def slot(i, p, c, et, prev, more):
                        if more and c == NC - 1 and et == 1:
                            load_out(i + 1, 1 - p)
                            store_c(i + 1)
                            for k in range(NC - 2):
                                spread_c(i + 1, k)
                            load_in(i + 2)
                            for k in range(NC - 2, NC):
                                spread_c(i + 1, k)

                    pairs(sp, prologue, slot, lambda: None)

                @block.tensor
                def _(pe):
                    def mean_square(i):
                        pe.wait_ge(s_sq, i + 1)
                        pe.matmul(bank_a, ones[:, :], sq[:, :], start=True, stop=True).then_inc(s_ms, 1)

                    def inner_products(i):
                        pe.wait_ge(s_wi, i * 16 + 16)
                        pe.wait_ge(s_xr, i + 1)
                        for et in range(ET):
                            pe.matmul(bank_of[et], wi("in_w", et * 128, 128), xr[:, :], start=True, stop=True).then_inc(s_xi, 1)

                    def gate_products(i):
                        for et in range(ET):
                            pe.wait_ge(s_cv, i * ET + et + 1)
                            pe.matmul(bank_of[et], wi("in_w", EI + et * 128, 128), xr[:, :], start=True, stop=True).then_inc(s_z, 1)

                    def x_products(i, p):
                        pe.wait_ge(s_xb, i * ET + ET)
                        pe.wait_ge(s_zc, i * ET + ET)
                        for et in range(ET):
                            mm = pe.matmul(bank_c[0:32 + NS, :], wi("xp", et * XW, 32 + NS), xb[p][:, et, :], start=(et == 0), stop=(et == ET - 1))
                        mm.then_inc(s_xp, 1)
                        for k in range(NC):
                            for et in range(ET):
                                mm = pe.matmul(bank_a[0:CH, k * NS:(k + 1) * NS], xb[p][:, et, k * CH:(k + 1) * CH],
                                               wi("xp", et * XW + 32 + NS, NS), start=(et == 0), stop=(et == ET - 1))
                        mm.then_inc(s_xp, 1)

                    def dt_products(i):
                        pe.wait_ge(s_xpc, i * 3 + 2)
                        for et in range(ET):
                            pe.matmul(bank_of[et], wi("dt_w", et * 128, 128, R), dtr, start=True, stop=True).then_inc(s_dtp, 1)

                    def transposes(i, p, c):
                        if not (is0(i) and c == 0):
                            pe.wait_ge(s_su, i * NC + c)
                        if c == 0:
                            pe.wait_ge(s_u, i * ET + ET)
                        pe.sem_inc(s_passed["pe"], 1)
                        for et in range(ET):
                            mm = pe.transpose(ps_uT[:, et * 128:(et + 1) * 128], u[p][:, et, c * CH:(c + 1) * CH], ident[:, :])
                        mm.then_inc(s_uT, 1)

                    def out_products(i, p):
                        for et in range(ET):
                            pe.wait_ge(s_yg, i * ET + et + 1)
                            mm = pe.matmul(bank_a, wo(p, "out_w", et * D, D), sz[p][:, et, :], start=(et == 0), stop=(et == ET - 1))
                        mm.then_inc(s_op, 1)

                    def prologue():
                        pe.wait_ge(s_c, 16 * 5)
                        for c in range(NB):
                            pe.matmul(ps[:, c, :], ones[:, :], x[:, c, :], start=True, stop=True).then_inc(s_mean, 1)
                        for c in range(NB):
                            pe.wait_ge(s_lnsq, c + 1)
                            pe.matmul(ps[:, NB + c, :], ones[:, :], ln_sq(c), start=True, stop=True).then_inc(s_lnvar, 1)
                        pe.wait_ge(s_a, NB)
                        mean_square(0)
                        inner_products(0)
                        gate_products(0)
                        x_products(0, 0)
                        dt_products(0)
                        transposes(0, 0, 0)
                        pe.wait_ge(s_xpc, 3)
                        mean_square(1)

                    def slot(i, p, c, et, prev, more):
                        k, n = c * ET + et, i + 1
                        q = i * NC + c
                        if et == 0:
                            pe.wait_ge(s_su, q + 1)
                            pe.wait_ge(s_g, q + 1)
                            if c < NC - 1:
                                transposes(i, p, c + 1)
                                pe.matmul(ps_carry, g[c % 2][:, :, CH - 1], su[c % 2][:, :], start=True, stop=True).then_inc(s_ca, 1)
                            elif more:
                                transposes(n, 1 - p, 0)
                        if not (is0(i) and c == 0):
                            pe.wait_ge(s_scan, (q - 1) * ET + et + 1)
                        for b in range(2):
                            mm = pe.matmul(ps_v_half[et][b], su[c % 2][:, et * 128:(et + 1) * 128],
                                           g[c % 2][:, b * NS // 2:(b + 1) * NS // 2, :], start=True, stop=True)
                        mm.then_inc(s_v, 1)
                        if more and k == 0:
                            inner_products(n)
                        if prev and k == 2:
                            out_products(i - 1, 1 - p)
                        if more and k == 3:
                            gate_products(n)
                        if more and k == 6:
                            if prev:
                                pe.wait_ge(s_res, i)
                            x_products(n, 1 - p)
                        if more and k == 8:
                            dt_products(n)
                        if more and k == 13:
                            pe.wait_ge(s_xpc, n * 3 + 3)
                            mean_square(n + 1)

                    pairs(pe, prologue, slot, lambda: out_products(PAIRS - 1, 1))

                @block.scalar
                def _(act):
                    def squares(i):
                        if not is0(i):
                            act.wait_ge(s_delta, i * ET)
                        if not (isinstance(i, int) and i < NB):
                            act.wait_ge(s_res, i - NB + 1 if isinstance(i, int) else i - 2)
                        act.activation(sq[:, :].unsqueeze(1), a[:, bass.ds(i & (NB - 1), 1), :], ACT.Square).then_inc(s_sq, 1)

                    def rstd(i):
                        act.wait_ge(s_ms, i + 1)
                        act.activation(rs[:, :], bank_a, ACT.Ln, bias=eps[:, 0:1]).then_inc(s_log, 1)
                        act.wait_ge(s_log, i + 1)
                        act.activation(rs[:, :], rs[:, :], ACT.Exp, scale=-0.5).then_inc(s_rs, 1)

                    def copy_inner(i):
                        for et in range(ET):
                            act.wait_ge(s_xi, i * ET + et + 1)
                            act.activation(cv[et][:, KC - 1:KC - 1 + L], bank_of[et], ACT.Copy).then_inc(s_cv, 1)

                    def a_exp(i):
                        act.wait_ge(s_wi, i * 16 + 16)
                        act.activation(aexp[:, :], wi("a_log", 0, ET * NS), ACT.Exp).then_inc(s_al, 1)

                    def sigmoid(dst, src, step, count):
                        act.activation(dst, src, ACT.Exp, scale=-1.0).then_inc(step, 1)
                        act.wait_ge(step, count + 1)
                        act.activation(dst, dst, ACT.Ln, bias=1.0).then_inc(step, 1)
                        act.wait_ge(step, count + 2)
                        return act.activation(dst, dst, ACT.Exp, scale=-1.0)

                    def conv_sigmoid(i, et):
                        act.wait_ge(s_cd, (i * ET + et + 1) * KC)
                        sigmoid(sig[et][:, :], conv[et][:, :], s_cst, (i * ET + et) * 2).then_inc(s_cs, 1)

                    def copy_gates(i, p, prev):
                        if prev:
                            act.wait_ge(s_op, i - 1)
                        for et in range(ET):
                            act.wait_ge(s_z, i * ET + et + 1)
                            act.activation(sz[p][:, et, :], bank_of[et], ACT.Copy).then_inc(s_zc, 1)

                    def gate_sigmoid(i, p, et):
                        act.wait_ge(s_zc, i * ET + et + 1)
                        sigmoid(sig[et][:, :], sz[p][:, et, :], s_zs, (i * ET + et) * 2).then_inc(s_zsig, 1)

                    def copy_x_products(i, p):
                        act.wait_ge(s_xp, i * 2 + 1)
                        act.activation(dtr, bank_c[0:R, :], ACT.Copy).then_inc(s_xpc, 1)
                        if not is0(i):
                            act.wait_ge(s_cs_st, i * 16)
                        act.activation(csb, bank_c[32:32 + NS, :], ACT.Copy).then_inc(s_xpc, 1)
                        act.wait_ge(s_xp, i * 2 + 2)
                        act.activation(bt[p][:, :, :], bank_a[0:CH, 0:NC * NS].rearrange("p (c n) -> p c n", n=NS), ACT.Copy)\
                           .then_inc(s_xpc, 1)

                    def softplus(i, et):
                        act.wait_ge(s_dtp, i * ET + et + 1)
                        if et:
                            act.wait_ge(s_delta, i * ET + et)
                        act.activation(mag[:, :], bank_of[et], ACT.Abs, bias=wi("dt_b", et)).then_inc(s_mag, 1)
                        act.wait_ge(s_mag, i * ET + et + 1)
                        act.activation(ex[:, :], mag[:, :], ACT.Exp, scale=-1.0).then_inc(s_ex, 1)
                        act.wait_ge(s_ex, i * ET + et + 1)
                        act.activation(lg[:, :], ex[:, :], ACT.Ln, bias=1.0).then_inc(s_sp, 1)
                        act.activation(lin[et][:, :], bank_of[et], ACT.Relu, bias=wi("dt_b", et)).then_inc(s_sp, 1)

                    def decays(i, p, half, first, last):
                        for m in range(first, last):
                            et, n = m // NS, m % NS
                            act.activation(decay[:, half, et, :, n, :],
                                           delta[:, et, half * L // 2:(half + 1) * L // 2].rearrange("p (c t) -> p c t", t=CH),
                                           ACT.Exp, scale=aneg[p][:, m:m + 1]).then_inc(s_da, 1)

                    def scan_inputs(i, p, c):
                        act.wait_ge(s_uT, i * NC + c + 1)
                        if c:
                            act.wait_ge(s_ca, i * (NC - 1) + c)
                        if not (is0(i) and c < 2):
                            act.wait_ge(s_v, (i * NC + c - 1) * ET)
                        act.activation(su[c % 2][0:CH, :], ps_uT, ACT.Copy)
                        carried = zeros if c == 0 else ps_carry
                        act.activation(su[c % 2][CH:CH + NS, :], carried, ACT.Copy).then_inc(s_su, 1)

                    def prologue():
                        act.preload_act_table_set(TABLES)
                        act.wait_ge(s_init, 3)
                        act.wait_ge(s_eps, 1)
                        for c in range(NB):
                            act.wait_ge(s_lnx, c + 1)
                            act.activation(ln_sq(c), ln_x(c), ACT.Square).then_inc(s_lnsq, 1)
                        for c in range(NB):
                            act.wait_ge(s_lnvar, c + 1)
                            act.activation(ln_rs(c), ps[:, NB + c, :], ACT.Ln, bias=eps[:, 0:1]).then_inc(s_lnlog, 1)
                        for c in range(NB):
                            act.wait_ge(s_lnlog, c + 1)
                            act.activation(ln_rs(c), ln_rs(c), ACT.Exp, scale=-0.5).then_inc(s_lnrs, 1)
                        act.wait_ge(s_a, NB)
                        squares(0)
                        rstd(0)
                        copy_inner(0)
                        a_exp(0)
                        copy_gates(0, 0, False)
                        for et in range(ET):
                            conv_sigmoid(0, et)
                        copy_x_products(0, 0)
                        for et in range(ET):
                            softplus(0, et)
                        scan_inputs(0, 0, 0)
                        act.wait_ge(s_delta, ET)
                        act.wait_ge(s_an, 1)
                        decays(0, 0, 0, 0, ET * NS)
                        squares(1)
                        rstd(1)

                    second = [8, 5, 8, 2, 2, 4, 3]
                    first = {11: 8, 12: 8, 13: 8, 14: 8}

                    def slot(i, p, c, et, prev, more):
                        k, n = c * ET + et, i + 1
                        if et == 0:
                            if c < NC - 1:
                                scan_inputs(i, p, c + 1)
                            elif more:
                                scan_inputs(n, 1 - p, 0)
                        if more and k == 1:
                            copy_inner(n)
                        if more and k == 3:
                            conv_sigmoid(n, 0)
                        if more and k == 4:
                            conv_sigmoid(n, 1)
                        if more and k == 5:
                            copy_gates(n, 1 - p, prev)
                            a_exp(n)
                        if more and k == 7:
                            copy_x_products(n, 1 - p)
                        if k in (7, 8):
                            gate_sigmoid(i, p, k - 7)
                        if more and k in (9, 10):
                            softplus(n, k - 9)
                        if k < len(second):
                            if k == 0 and not is0(i):
                                act.wait_ge(s_scan, i * UN)
                            decays(i, p, 1, sum(second[:k]), sum(second[:k + 1]))
                        if more and k in first:
                            if k == 11:
                                act.wait_ge(s_an, n + 1)
                                act.wait_ge(s_scan, i * UN + UN // 2)
                            done = sum(v for s, v in first.items() if s < k)
                            act.wait_ge(s_delta, n * ET + 1 + done // NS)
                            decays(n, 1 - p, 0, done, done + first[k])
                        if more and k == 12:
                            squares(n + 1)
                        if more and k == 14:
                            rstd(n + 1)

                    pairs(act, prologue, slot, lambda: None)

                @block.gpsimd
                def _(pool):
                    def kernel_of(i, p, c):
                        if c == 0:
                            pool.wait_ge(s_xpc, i * 3 + 3)
                        if not (is0(i) and c < 2):
                            pool.wait_ge(s_v, (i * NC + c - 1) * ET)
                        if c > 1:
                            pool.wait_ge(s_ca, i * (NC - 1) + c - 1)
                        elif c == 0 and not is0(i):
                            pool.wait_ge(s_ca, i * (NC - 1))
                        pool.tensor_tensor(g[c % 2][0:CH, :, :], kern[:, :].unsqueeze(1).broadcast_to([CH, NS, CH]),
                                           bt[p][:, c, :].unsqueeze(2).broadcast_to([CH, NS, CH]), ALU.mult).then_inc(s_g, 1)

                    def first_decays(i, half):
                        pool.wait_ge(s_da, (i * 2 + half + 1) * ET * NS)
                        pool.sem_inc(s_passed["pool"], 1)
                        d0 = decay[:, half, :, :, :, 0].rearrange("p e c n -> p (e c n)")
                        pool.tensor_copy(decay0[:, half, :, :, :].rearrange("p e c n -> p (e c n)"), d0).then_inc(s_d0c, 1)
                        pool.wait_ge(s_d0c, i * 2 + half + 1)
                        pool.sem_inc(s_passed["pool"], 1)
                        pool.memset(d0, 0.0).then_inc(s_d0, 1)

                    def times_c(i, c, et):
                        if et == 0:
                            pool.wait_ge(s_cb[c], i * 16 + 16)
                        pool.wait_ge(s_scan, (i * NC + c) * ET + et + 1)
                        if not (is0(i) and c < 2):
                            pool.wait_ge(s_y, (i * NC + c - 2) * ET + et + 1)
                        pool.tensor_tensor(hc[(c % 2) * ET + et][:, :, :], h[et][:, :, :], cb[:, c, :, :], ALU.mult).then_inc(s_hc, 1)

                    def prologue():
                        pool.memset(zeros, 0.0).then_inc(s_init, 1)
                        pool.wait_ge(s_init, 1)
                        for et in range(ET):
                            pool.memset(cv[et][:, 0:KC - 1], 0.0).then_inc(s_init, 1)
                        pool.wait_ge(s_c, 16 * 5)
                        kernel_of(0, 0, 0)
                        first_decays(0, 0)

                    def slot(i, p, c, et, prev, more):
                        if et == 0:
                            if c < NC - 1:
                                kernel_of(i, p, c + 1)
                            elif more:
                                kernel_of(i + 1, 1 - p, 0)
                        if c * ET + et == 7:
                            first_decays(i, 1)
                        times_c(i, c, et)
                        if et == 0 and c == NC - 1 and more:
                            first_decays(i + 1, 0)

                    pairs(pool, prologue, slot, lambda: None)

                @block.vector
                def _(dve):
                    def normed(i):
                        dve.wait_ge(s_rs, i + 1)
                        dve.wait_ge(s_wi, i * 16 + 16)
                        dve.scalar_tensor_tensor(xr[:, :].unsqueeze(1), a[:, bass.ds(i & (NB - 1), 1), :], wi("norm_w"),
                                                 rs[:, :].unsqueeze(1), ALU.mult, ALU.mult).then_inc(s_xr, 1)

                    def convolution(i, et):
                        dve.wait_ge(s_cv, i * ET + et + 1)
                        if not is0(i):
                            dve.wait_ge(s_delta, i * ET)
                        dve.tensor_scalar(conv[et][:, :], cv[et][:, 0:L], wi("conv_w", et * KC), wi("conv_b", et),
                                          ALU.mult, ALU.add).then_inc(s_cd, 1)
                        for k in range(1, KC):
                            dve.wait_ge(s_cd, (i * ET + et) * KC + k)
                            dve.scalar_tensor_tensor(conv[et][:, :], cv[et][:, k:k + L], wi("conv_w", et * KC + k), conv[et][:, :],
                                                     ALU.mult, ALU.add).then_inc(s_cd, 1)

                    def inner_silu(i, p, et):
                        dve.wait_ge(s_cs, i * ET + et + 1)
                        dve.tensor_tensor(xb[p][:, et, :], conv[et][:, :], sig[et][:, :], ALU.mult).then_inc(s_xb, 1)

                    def gate_silu(i, p, et):
                        dve.wait_ge(s_zsig, i * ET + et + 1)
                        dve.tensor_tensor(sz[p][:, et, :], sz[p][:, et, :], sig[et][:, :], ALU.mult).then_inc(s_sz, 1)

                    def negative_a(i, p):
                        dve.wait_ge(s_al, i + 1)
                        if not (isinstance(i, int) and i < 2):
                            dve.wait_ge(s_da, (i - 1) * 2 * ET * NS)
                        dve.tensor_scalar(aneg[p][:, :], aexp[:, :], -1.0, None, ALU.mult).then_inc(s_an, 1)

                    def softplus(i, p, et):
                        n = (i * ET + et) * 6
                        dve.wait_ge(s_ex, i * ET + et + 1)
                        dve.tensor_scalar(sig[et][:, :], ex[:, :], SMALL, None, ALU.is_lt).then_inc(s_sd, 1)
                        dve.tensor_scalar(mag[:, :], ex[:, :], -1.0 / 4, 1.0 / 3, ALU.mult, ALU.add).then_inc(s_sd, 1)
                        dve.wait_ge(s_sd, n + 2)
                        dve.tensor_tensor(mag[:, :], mag[:, :], ex[:, :], ALU.mult).then_inc(s_sd, 1)
                        dve.wait_ge(s_sd, n + 3)
                        dve.scalar_tensor_tensor(mag[:, :], mag[:, :], -0.5, ex[:, :], ALU.add, ALU.mult).then_inc(s_sd, 1)
                        dve.wait_ge(s_sd, n + 4)
                        dve.scalar_tensor_tensor(mag[:, :], mag[:, :], 1.0, ex[:, :], ALU.add, ALU.mult).then_inc(s_sd, 1)
                        dve.wait_ge(s_sd, n + 5)
                        dve.wait_ge(s_sp, (i * ET + et) * 2 + 1)
                        dve.sem_inc(s_passed["dve"], 1)
                        dve.copy_predicated(lg[:, :], sig[et][:, :].bitcast(mybir.dt.uint32), mag[:, :]).then_inc(s_sd, 1)
                        dve.wait_ge(s_sd, n + 6)
                        dve.wait_ge(s_sp, (i * ET + et) * 2 + 2)
                        if et == 0 and not is0(i):
                            dve.wait_ge(s_da, i * 2 * ET * NS)
                        dve.tensor_tensor(delta[:, et, :], lin[et][:, :], lg[:, :], ALU.add).then_inc(s_delta, 1)
                        dve.wait_ge(s_delta, i * ET + et + 1)
                        dve.tensor_tensor(u[p][:, et, :], delta[:, et, :], xb[p][:, et, :], ALU.mult).then_inc(s_u, 1)

                    def reduce_states(i, c, et):
                        dve.wait_ge(s_hc, (i * NC + c) * ET + et + 1)
                        dve.tensor_reduce(y[:, et, c * CH:(c + 1) * CH], hc[(c % 2) * ET + et][:, :, :].rearrange("p n t -> p t n"),
                                          AX.X, ALU.add).then_inc(s_y, 1)

                    def gated_output(i, p, et):
                        dve.wait_ge(s_y, (i * NC + NC - 1) * ET + et + 1)
                        dve.wait_ge(s_wo[p], (i // 2) * 16 + 16 if isinstance(i, int) else (i >> 1) * 16 + 16)
                        dve.scalar_tensor_tensor(xb[p][:, et, :], xb[p][:, et, :], wo(p, "dp", et), y[:, et, :], ALU.mult, ALU.add)\
                           .then_inc(s_yd, 1)
                        dve.wait_ge(s_yd, i * ET + et + 1)
                        dve.tensor_tensor(sz[p][:, et, :], xb[p][:, et, :], sz[p][:, et, :], ALU.mult).then_inc(s_yg, 1)

                    def residual(i):
                        dve.wait_ge(s_op, i + 1)
                        at = bass.ds(i & (NB - 1), 1)
                        dve.tensor_tensor(a[:, at, :], a[:, at, :], bank_a.unsqueeze(1), ALU.add).then_inc(s_res, 1)

                    def prologue():
                        dve.memset(eps[:, :], EPS).then_inc(s_eps, 1)
                        for c in range(NB):
                            dve.wait_ge(s_mean, c + 1)
                            dve.tensor_tensor(ln_x(c), x[:, c, :], ps[:, c, :], ALU.subtract).then_inc(s_lnx, 1)
                        for c in range(NB):
                            dve.wait_ge(s_lnx, c + 1)
                            dve.wait_ge(s_lnrs, c + 1)
                            dve.tensor_tensor(a[:, c, :], ln_x(c), ln_rs(c), ALU.mult).then_inc(s_a, 1)
                        dve.wait_ge(s_a, NB)
                        normed(0)
                        for et in range(ET):
                            convolution(0, et)
                        negative_a(0, 0)
                        for et in range(ET):
                            inner_silu(0, 0, et)
                        for et in range(ET):
                            softplus(0, 0, et)
                        normed(1)

                    def slot(i, p, c, et, prev, more):
                        k, n = c * ET + et, i + 1
                        un = i * UN + k
                        half, ch = c // HC, c % HC
                        if k % (UN // 2) == 0:
                            dve.wait_ge(s_d0, i * 2 + half + 1)
                        if c:
                            t = i * (NC - 1) * ET * 2 + ((c - 1) * ET + et) * 2
                            dve.wait_ge(s_scan, un - 1)
                            dve.tensor_tensor(carry_in[:, :], decay0[:, half, et, ch, :], h[et][:, :, CH - 1], ALU.mult).then_inc(s_t0, 1)
                            reduce_states(i, c - 1, et)
                            dve.wait_ge(s_t0, t + 1)
                            dve.wait_ge(s_v, un + 1)
                            dve.tensor_tensor(ps_v[et][:, :, 0], ps_v[et][:, :, 0], carry_in[:, :], ALU.add).then_inc(s_t0, 1)
                            dve.wait_ge(s_t0, t + 2)
                        elif prev:
                            reduce_states(i - 1, NC - 1, et)
                        dve.wait_ge(s_v, un + 1)
                        if not (is0(i) and c == 0):
                            dve.wait_ge(s_hc, un - 1)
                        dve.tensor_tensor_scan(h[et][:, :, :].rearrange("p n t -> p (n t)"),
                                               decay[:, half, et, ch, :, :].rearrange("p n t -> p (n t)"),
                                               ps_v[et].rearrange("p n t -> p (n t)"), 0.0, ALU.mult, ALU.add).then_inc(s_scan, 1)
                        if prev and k == 1:
                            for e2 in range(ET):
                                gated_output(i - 1, 1 - p, e2)
                        if more and k in (2, 3):
                            convolution(n, k - 2)
                        if prev and k == 3:
                            residual(i - 1)
                        if more and k in (4, 5):
                            inner_silu(n, 1 - p, k - 4)
                        if more and k == 6:
                            negative_a(n, 1 - p)
                        if k in (8, 9):
                            gate_silu(i, p, k - 8)
                        if more and k in (10, 11):
                            softplus(n, 1 - p, k - 10)
                        if more and k == 15:
                            if not (isinstance(i, int) and i == PAIRS - 2):
                                normed(n + 1)

                    def epilogue():
                        for et in range(ET):
                            reduce_states(PAIRS - 1, NC - 1, et)
                        for et in range(ET):
                            gated_output(PAIRS - 1, 1, et)
                        residual(PAIRS - 1)
                        dve.wait_ge(s_res, PAIRS)
                        dve.tensor_tensor(x[:, :, :], x[:, :, :], a[:, :, :], ALU.add).then_inc(s_end, 1)
                        dve.wait_ge(s_end, 1)

                    pairs(dve, prologue, slot, epilogue)


def macaron(nc, dram):
    with ExitStack() as ctx:
        x = ctx.enter_context(nc.sbuf_tensor("x_res", [D, NB, L], F32))
        Ffn(nc, x, dram["x"], None, dram, None, "f1").build()
        Mamba(nc, x, dram).build()
        Ffn(nc, x, None, dram["out"], dram, None, "f2").build()


def kernel(**inputs):
    import concourse.bacc as _bacc
    from concourse.bass_utils import run_bass_kernel_spmd as _run

    f = {k.replace("L0_attn_", "m_").replace("L0_ffn_", "f_"): np.asarray(v) for k, v in inputs.items()}
    lay = np.ascontiguousarray
    arrays = {
        "x": lay(f["m_x"].reshape(NB, L, D).transpose(2, 0, 1)),
        "w1": lay(f["f_W1"].reshape(E, D, FT, 128).transpose(1, 0, 2, 3).reshape(D, S1, 128)),
        "w2": lay(f["f_W2"].reshape(E, FT, 128, D).transpose(2, 0, 1, 3).reshape(128, S1, D)),
        "b1": lay(f["f_b1"].reshape(S1, 128).T),
        "b2": lay(f["f_b2"].T),
        "wr": lay(f["f_Wr"]),
        "br": lay(np.broadcast_to(f["f_br"][None, :], (128, E))),
    }
    def tiles(v):
        return v.reshape(NL, ET, 128, -1).transpose(0, 2, 1, 3).reshape(NL, 128, -1)

    xp = f["m_x_proj_w"].transpose(0, 2, 1)
    dt_w = np.zeros((NL, 128, EI), np.float32)
    dt_w[:, :R, :] = f["m_dt_w"].transpose(0, 2, 1)
    parts = {
        "in_w": f["m_in_proj_w"].transpose(0, 2, 1),
        "xp": tiles(np.concatenate([xp[:, :, :R], np.zeros((NL, EI, 32 - R), np.float32), xp[:, :, R + NS:], xp[:, :, R:R + NS]], axis=2)),
        "out_w": tiles(f["m_out_w"].transpose(0, 2, 1)),
        "conv_w": tiles(f["m_conv_w"]),
        "conv_b": tiles(f["m_conv_b"]),
        "dt_b": tiles(f["m_dt_b"]),
        "a_log": tiles(f["m_A_log"]),
        "dp": tiles(f["m_Dp"]),
        "norm_w": f["m_norm_w"].reshape(NL, D, 1),
        "dt_w": dt_w,
    }
    arrays["w_in"] = lay(np.concatenate([parts[n] for n, _ in PACK_IN], axis=2))
    arrays["w_out"] = lay(np.concatenate([parts[n] for n, _ in PACK_OUT], axis=2))
    t = np.arange(CH)
    arrays["ones"] = np.full((128, 128), 1.0 / D, np.float32)
    arrays["ident"] = np.eye(128, dtype=np.float32)
    arrays["sel"] = lay(np.broadcast_to(np.eye(E, dtype=np.float32)[:, :, None], (E, E, 128)))
    lag = t[None, :] - t[:, None]
    arrays["kern"] = np.where(lag >= 0, BETA ** np.maximum(lag, 0).astype(np.float64), 0.0).astype(np.float32)
    arrays["carry_kern"] = (np.eye(NS)[:, :, None] * BETA ** (t + 1.0)[None, None, :]).astype(np.float32)

    nc = _bacc.Bacc("TRN2", target_bir_lowering=False, num_devices=1)
    dram = {n: nc.dram_tensor(f"in_{n}", v.shape, F32, kind="ExternalInput").ap() for n, v in arrays.items()}
    dram["out"] = nc.dram_tensor("out_x", (D, NB, L), F32, kind="ExternalOutput").ap()
    dram["c_scratch"] = nc.dram_tensor("c_scratch", (NC, NS, CH), F32, kind="Internal").ap()
    macaron(nc, dram)
    r = _run(nc, [{f"in_{n}": v for n, v in arrays.items()}], core_ids=[0])
    return lay(np.asarray(r.results[0]["out_x"]).transpose(1, 2, 0))
```

```python
from contextlib import ExitStack

import concourse.bass as bass
import numpy as np
from concourse import mybir

F32 = mybir.dt.float32
F32R = mybir.dt.float32r
ALU = mybir.AluOpType
ACT = mybir.ActivationFunctionType
AX = mybir.AxisListType
TABLES = "natural_log_exp_and_others"

D = 128
NB = 4
L = 512
E = 8
F = 512
FT = F // 128
S1 = E * FT
TT = L // 128
EI = 256
ET = EI // 128
NS = 16
R = 8
KC = 4
NL = 2
CH = 64
NC = L // CH
UN = NC * ET
HC = NC // 2
BETA = 0.6
EPS = 1e-5
ITERS = 25
SMALL = 1.0 / 32

XW = 32 + 2 * NS
PACK_IN = [("in_w", 2 * EI), ("xp", ET * XW), ("conv_w", ET * KC), ("conv_b", ET), ("dt_b", ET),
           ("a_log", ET * NS), ("norm_w", 1), ("dt_w", EI)]
PACK_OUT = [("out_w", ET * D), ("dp", ET)]


def columns(pack):
    at, col = 0, {}
    for name, n in pack:
        col[name] = at
        at += n
    return col, at


COL_IN, NW_IN = columns(PACK_IN)
COL_OUT, NW_OUT = columns(PACK_OUT)


class Ffn:

    def __init__(self, nc, x, ones, ident, src, out, dram, tag):
        self.nc, self.x, self.src, self.out, self.dram, self.tag = nc, x, src, out, dram, tag
        self.ones, self.ident = ones, ident

    def build(self):
        nc, x, tag, dram, ones, ident = self.nc, self.x, self.tag, self.dram, self.ones, self.ident
        LAG = 3
        RING = 4
        G = NB * TT
        HALF = S1 // 2
        VEC = range(HALF + 1, S1 - LAG - 1, 2)
        AHEAD = 2 * E
        with ExitStack() as ctx:
            def sb(name, shape, dtype=F32):
                return ctx.enter_context(nc.sbuf_tensor(f"{name}_{tag}", shape, dtype))

            def sem(name):
                return ctx.enter_context(nc.semaphore(f"{name}_{tag}"))

            ps = ctx.enter_context(nc.psum_tensor(f"ps_{tag}", [128, 8, 512], F32))
            ps_hidden = [ps[:, 0, :], ps[:, 1, :]]
            ps_y = [ps[:, 2, :], ps[:, 3, :]]
            ps_gate = [ps[:, 4, :], ps[:, 5, :]]
            ps_logit = ps[:, 7, 0:G * E]
            ps_gT = ps[0:E, 7, :]

            w = [sb("w1", [D, S1, 128]), sb("w2", [128, S1, D])]
            wh = [sb(f"w{m + 1}_high", [128, S1, 128], F32R) for m in range(2)]
            wl = [sb(f"w{m + 1}_low", [128, S1, 128], F32R) for m in range(2)]
            b1 = sb("b1", [128, S1])
            b2 = sb("b2", [D, E])
            wr = sb("wr", [D, E])
            br = sb("br", [128, E])
            sel = sb("sel", [E, E, 128])
            selr = sb("sel_r", [E, E, 128], F32R)
            eps = sb("eps", [128, 1])
            xn = sb("xn", [D, NB, L])
            xh = sb("xn_high", [D, NB, L], F32R)
            xl = sb("xn_low", [D, NB, L], F32R)
            hf = sb("hidden", [128, RING, L])
            hh = sb("hidden_high", [128, RING, L], F32R)
            hl = sb("hidden_low", [128, RING, L], F32R)
            yb = sb("yb", [D, 2 * E, L])
            prod = sb("prod", [D, 2, L])
            acc = sb("acc", [D, L])
            xs = sb("xs", [128, G, E])
            z = sb("z", [128, G, E])
            z2 = sb("z2", [128, G, E])
            gates = sb("gates", [128, G, E])
            mx = sb("mx", [128, G])
            lo = sb("lo", [128, G])
            dm = sb("dm", [128, G])
            tau = sb("tau", [128, G])
            f_lo = sb("f_lo", [128, G])
            f_m = sb("f_m", [128, G])
            step = sb("step", [128, G])
            g_tok = sb("gates_of_batch", [128, TT, E])
            gh = sb("gates_high", [E, L], F32R)
            gl = sb("gates_low", [E, L], F32R)

            s_x = [sem(f"x{c}_loaded") for c in range(NB)] if self.src is not None else None
            s_ones = sem("ones_loaded") if self.src is not None else None
            s_c = sem("constants_loaded")
            s_w = [sem(f"w_{e}_loaded") for e in range(E)]
            s_mean = sem("mean_ready")
            s_xc = sem("centred_ready")
            s_sq = sem("squares_ready")
            s_var = sem("variance_ready")
            s_rs = sem("rstd_step")
            s_xn = sem("normed_ready")
            s_part = sem("part_split")
            s_ws = sem("weights_split")
            s_xsp = sem("normed_split")
            s_sel = sem("selectors_ready")
            s_eps = sem("eps_filled")
            s_log = sem("logits_ready")
            s_dve = sem("gating_step_done")
            s_gates = sem("gates_ready")
            s_gtok = sem("gates_of_batch_ready")
            s_gt = sem("gates_transposed")
            s_gth = sem("gates_high_copied")
            s_gtc = sem("gates_copied")
            s_gb = sem("gate_broadcast")
            s_mm1 = sem("hidden_product_ready")
            s_hf = sem("hidden_ready")
            s_hlp = sem("hidden_low_by_pool_ready")
            s_hld = sem("hidden_low_by_vector_ready")
            s_mm2 = sem("hidden_used")
            s_y = sem("expert_output_copied")
            s_prod = sem("gated_output_ready")
            s_acc = sem("gated_sum_ready")
            s_new = sem("x_updated")
            s_out = sem("x_stored") if self.out is not None else None
            s_passed = sem("wait_passed_pe")

            def is0(c):
                return isinstance(c, int) and c == 0

            def low_wait(eng, c, s):
                mine = S1 - len(VEC)
                if is0(c):
                    eng.wait_ge(s_hlp, s + 1)
                elif s > VEC[-1]:
                    eng.wait_ge(s_hlp, c * mine + s + 1)
                elif s in VEC:
                    eng.wait_ge(s_hld, (c - 1) * len(VEC) + VEC.index(s) + 1)
                else:
                    eng.wait_ge(s_hlp, (c - 1) * mine + S1 + s + 1 - sum(v < s for v in VEC))

            def low_part(eng, c, s, ready):
                eng.wait_ge(s_hf, (c * S1 + s + 1) * 2)
                if not (is0(c) and s < RING):
                    eng.wait_ge(s_mm2, c * S1 + s + 1 - RING)
                eng.tensor_tensor(hl[:, s % RING, :], hf[:, s % RING, :], hh[:, s % RING, :].bitcast(F32), ALU.subtract)\
                   .then_inc(ready, 1)

            OWN_GATES = E + 2

            def own_step(e):
                return max(OWN_GATES + 2 + e, e * FT + FT + LAG + 2)

            with nc.Block() as block:
                @block.sync
                def _(sp):
                    if self.src is not None:
                        sp.dma_start(ones[:, :], dram["ones"]).then_inc(s_ones, 16)
                        for c in range(NB):
                            sp.dma_start(x[:, c, :], self.src[:, c, :]).then_inc(s_x[c], 16)
                        sp.dma_start(ident[:, :], dram["ident"]).then_inc(s_ones, 16)
                    for t, name in ((wr, "wr"), (br, "br"), (sel, "sel"), (b1, "b1"), (b2, "b2")):
                        sp.dma_start(t[tuple([slice(None)] * len(t.shape))], dram[name]).then_inc(s_c, 16)
                    for e in range(E):
                        for m in range(2):
                            sp.dma_start(w[m][:, e * FT:(e + 1) * FT, :], dram[f"w{m + 1}"][:, e * FT:(e + 1) * FT, :]).then_inc(s_w[e], 16)
                    if self.out is not None:
                        for c in range(NB):
                            sp.wait_ge(s_new, c + 2)
                            sp.dma_start(self.out[:, c, :], x[:, c, :]).then_inc(s_out, 16)
                        sp.wait_ge(s_out, 16 * NB)

                @block.tensor
                def _(pe):
                    if self.src is not None:
                        pe.wait_ge(s_ones, 32)
                    for c in range(NB):
                        if self.src is not None:
                            pe.wait_ge(s_x[c], 16)
                        pe.matmul(ps[:, c, :], ones[:, :], x[:, c, :], start=True, stop=True).then_inc(s_mean, 1)
                    for c in range(NB):
                        pe.wait_ge(s_sq, c + 1)
                        pe.matmul(ps[:, NB + c, :], ones[:, :], hf[:, c, :], start=True, stop=True).then_inc(s_var, 1)
                    pe.wait_ge(s_xn, NB)
                    pe.wait_ge(s_c, 16 * 5)
                    for t in range(G):
                        mm = pe.matmul(ps_logit[:, t * E:(t + 1) * E], xn[:, t // TT, (t % TT) * 128:(t % TT + 1) * 128], wr[:, :],
                                       start=True, stop=True)
                    mm.then_inc(s_log, 1)

                    def hidden_product(c, s):
                        if is0(c) and s % FT == 0:
                            pe.wait_ge(s_ws, s // FT + 1)
                        if is0(c) and s == 0:
                            pe.wait_ge(s_xsp, 1)
                        if not (is0(c) and s < 2):
                            pe.wait_ge(s_hf, (c * S1 + s - 1) * 2)
                            pe.sem_inc(s_passed, 1)
                        at = bass.ds(c, 1)
                        pe.matmul(ps_hidden[s % 2], wh[0][:, s, :], xh[:, at, :], start=True, stop=False)
                        pe.matmul(ps_hidden[s % 2], wh[0][:, s, :], xl[:, at, :], start=False, stop=False)
                        pe.matmul(ps_hidden[s % 2], wl[0][:, s, :], xh[:, at, :], start=False, stop=True).then_inc(s_mm1, 1)

                    def expert_product(c, s):
                        e, f = s // FT, s % FT
                        if f == 0 and not (is0(c) and e < 2):
                            pe.wait_ge(s_y, c * E + e - 1)
                        low_wait(pe, c, s)
                        pe.matmul(ps_y[e % 2], wh[1][:, s, :], hh[:, s % RING, :], start=(f == 0), stop=False)
                        pe.matmul(ps_y[e % 2], wl[1][:, s, :], hh[:, s % RING, :], start=False, stop=False)
                        pe.matmul(ps_y[e % 2], wh[1][:, s, :], hl[:, s % RING, :], start=False, stop=(f == FT - 1)).then_inc(s_mm2, 1)

                    def gate_transposes(c):
                        pe.wait_ge(s_gtok, c + 1)
                        pe.sem_inc(s_passed, 1)
                        for t in range(TT):
                            mm = pe.transpose(ps_gT[:, t * 128:(t + 1) * 128], g_tok[:, t, :], ident[:, :])
                        mm.then_inc(s_gt, 1)

                    def gate_broadcast(c, e):
                        if e == 0:
                            pe.wait_ge(s_gtc, c + 1)
                        pe.wait_ge(s_prod, AHEAD + c * E + e - 1)
                        pe.sem_inc(s_passed, 1)
                        pe.matmul(ps_gate[e % 2], selr[:, e, :], gh[:, :], start=True, stop=False)
                        pe.matmul(ps_gate[e % 2], selr[:, e, :], gl[:, :], start=False, stop=True).then_inc(s_gb, 1)

                    def products(c, s):
                        hidden_product(c, s)
                        if s >= LAG:
                            expert_product(c, s - LAG)
                        elif not is0(c):
                            expert_product(c - 1, S1 + s - LAG)

                    for s in range(S1):
                        products(0, s)
                    pe.wait_ge(s_xsp, NB)
                    with pe.Fori(1, NB - 1) as c:
                        for s in range(S1):
                            if s == HALF - 2:
                                gate_transposes(c - 1)
                            products(c, s)
                            if s >= HALF and s % 2 == 0:
                                gate_broadcast(c - 1, (s - HALF) // 2)
                    gate_transposes(NB - 2)
                    for s in range(S1):
                        products(NB - 1, s)
                        if 1 <= s <= E:
                            gate_broadcast(NB - 2, s - 1)
                        if s == OWN_GATES:
                            gate_transposes(NB - 1)
                        for e in range(E):
                            if s == own_step(e) - 1:
                                gate_broadcast(NB - 1, e)
                    for s in range(S1, S1 + LAG):
                        expert_product(NB - 1, s - LAG)
                    for e in range(E):
                        if own_step(e) > S1:
                            gate_broadcast(NB - 1, e)

                @block.scalar
                def _(act):
                    act.preload_act_table_set(TABLES)
                    act.wait_ge(s_eps, 1)
                    for c in range(NB):
                        act.wait_ge(s_xc, c + 1)
                        act.activation(hf[:, c, :], yb[:, c, :], ACT.Square).then_inc(s_sq, 1)
                    for c in range(NB):
                        act.wait_ge(s_var, c + 1)
                        act.activation(yb[:, NB + c, :], ps[:, NB + c, :], ACT.Ln, bias=eps[:, 0:1]).then_inc(s_rs, 1)
                    for c in range(NB):
                        act.wait_ge(s_rs, c + 1)
                        act.activation(yb[:, NB + c, :], yb[:, NB + c, :], ACT.Exp, scale=-0.5).then_inc(s_rs, 1)

                    def relu(c, s):
                        act.wait_ge(s_mm1, c * S1 + s + 1)
                        if not (is0(c) and s < RING):
                            act.wait_ge(s_mm2, c * S1 + s + 1 - RING)
                        act.activation(hf[:, s % RING, :], ps_hidden[s % 2], ACT.Relu, bias=b1[:, s:s + 1]).then_inc(s_hf, 1)
                        act.activation(hh[:, s % RING, :], ps_hidden[s % 2], ACT.Relu, bias=b1[:, s:s + 1]).then_inc(s_hf, 1)

                    def expert_out(c, e):
                        act.wait_ge(s_mm2, c * S1 + (e + 1) * FT)
                        if not is0(c):
                            act.wait_ge(s_prod, AHEAD + (c - 2) * E + e + 1)
                        act.activation(yb[:, bass.ds((c & 1) * E + e, 1), :], ps_y[e % 2].unsqueeze(1), ACT.Identity, bias=b2[:, e:e + 1])\
                           .then_inc(s_y, 1)

                    def batch(c):
                        for s in range(S1):
                            relu(c, s)
                            if s > LAG and (s - LAG - 1) % FT == FT - 1:
                                expert_out(c, (s - LAG - 1) // FT)
                            if s == LAG and not is0(c):
                                expert_out(c - 1, E - 1)

                    act.wait_ge(s_c, 16 * 5)
                    batch(0)
                    with act.Fori(1, NB) as c:
                        batch(c)
                    expert_out(NB - 1, E - 1)

                @block.gpsimd
                def _(pool):
                    for s in range(S1):
                        low_part(pool, 0, s, s_hlp)
                    with pool.Fori(1, NB) as c:
                        for s in range(S1):
                            if s not in VEC:
                                low_part(pool, c, s, s_hlp)

                @block.vector
                def _(dve):
                    parts = [0]

                    def split(high, low, full, done):
                        def first():
                            dve.tensor_copy(high, full).then_inc(s_part, 1)
                            parts[0] += 1

                        def second():
                            dve.wait_ge(s_part, parts[0])
                            dve.tensor_tensor(low, full, high.bitcast(F32), ALU.subtract).then_inc(*done)
                        return [first, second]

                    def split_weights(e):
                        steps = []
                        for m in range(2):
                            at = slice(e * FT, (e + 1) * FT)
                            first, second = split(wh[m][:, at, :], wl[m][:, at, :], w[m][:, at, :], (s_ws, 1) if m else (s_part, 1))

                            def wait_then(first=first):
                                dve.wait_ge(s_w[e], 32)
                                first()

                            def and_count(second=second, m=m):
                                second()
                                parts[0] += 1 - m
                            steps += [wait_then, and_count]
                        return steps

                    def split_normed(c):
                        return split(xh[:, c, :], xl[:, c, :], xn[:, c, :], (s_xsp, 1))

                    dve.sem_inc(s_prod, AHEAD)
                    dve.sem_inc(s_new, 1)
                    dve.memset(eps[:, :], EPS).then_inc(s_eps, 1)
                    for c in range(NB):
                        dve.wait_ge(s_mean, c + 1)
                        dve.tensor_tensor(yb[:, c, :], x[:, c, :], ps[:, c, :], ALU.subtract).then_inc(s_xc, 1)
                    for c in range(NB):
                        dve.wait_ge(s_xc, c + 1)
                        dve.wait_ge(s_rs, NB + c + 1)
                        dve.tensor_tensor(xn[:, c, :], yb[:, c, :], yb[:, NB + c, :], ALU.mult).then_inc(s_xn, 1)
                    dve.wait_ge(s_xn, NB)
                    for op in split_normed(0) + split_weights(0):
                        op()

                    fillers = []
                    for e in range(1, E):
                        fillers += split_weights(e)
                    for c in range(1, NB):
                        fillers += split_normed(c)
                    done = [0]

                    def then(ins):
                        done[0] += 1
                        ins.then_inc(s_dve, 1)
                        if fillers:
                            fillers.pop(0)()
                        dve.wait_ge(s_dve, done[0])

                    def wide(t):
                        return t[:, :].unsqueeze(2).broadcast_to([128, G, E])

                    def power_sum(out, tau_ap):
                        then(dve.tensor_tensor(z[:, :, :], xs[:, :, :], tau_ap, ALU.subtract))
                        then(dve.scalar_tensor_tensor(z2[:, :, :], z[:, :, :], 0.0, z[:, :, :], ALU.max, ALU.mult))
                        then(dve.tensor_reduce(out[:, :], z2[:, :, :], AX.X, ALU.add))

                    dve.wait_ge(s_log, 1)
                    lg = ps_logit.rearrange("p (g e) -> p g e", e=E)
                    then(dve.tensor_tensor(z[:, :, :], lg, br[:, :].unsqueeze(1).broadcast_to([128, G, E]), ALU.add))
                    then(dve.tensor_scalar(xs[:, :, :], z[:, :, :], 0.5, None, ALU.mult))
                    then(dve.tensor_reduce(mx[:, :], xs[:, :, :], AX.X, ALU.max))
                    then(dve.tensor_scalar(lo[:, :], mx[:, :], -1.0, None, ALU.add))
                    then(dve.tensor_scalar(dm[:, :], mx[:, :], -float(np.float32((1.0 / E) ** 0.5)), None, ALU.add))
                    then(dve.tensor_tensor(dm[:, :], dm[:, :], lo[:, :], ALU.subtract))
                    power_sum(f_lo, wide(lo))
                    then(dve.tensor_scalar(f_lo[:, :], f_lo[:, :], -1.0, None, ALU.add))
                    for k in range(ITERS):
                        half = 0.5 ** (k + 1)
                        then(dve.scalar_tensor_tensor(tau[:, :], dm[:, :], half, lo[:, :], ALU.mult, ALU.add))
                        power_sum(f_m, wide(tau))
                        if k < ITERS - 1:
                            then(dve.scalar_tensor_tensor(step[:, :], f_m[:, :], -1.0, f_lo[:, :], ALU.add, ALU.mult))
                            then(dve.scalar_tensor_tensor(step[:, :], step[:, :], 0.0, dm[:, :], ALU.is_ge, ALU.mult))
                            then(dve.scalar_tensor_tensor(lo[:, :], step[:, :], half, lo[:, :], ALU.mult, ALU.add))
                    then(dve.reciprocal(step[:, :], f_m[:, :]))
                    then(dve.tensor_tensor(z[:, :, :], z2[:, :, :], wide(step), ALU.mult))
                    dve.scalar_tensor_tensor(gates[:, :, :], z[:, :, :], 1e-9, z[:, :, :], ALU.is_gt, ALU.mult).then_inc(s_gates, 1)

                    def gates_of(c):
                        dve.tensor_copy(g_tok[:, :, :], gates[:, bass.ds(c * TT, TT), :]).then_inc(s_gtok, 1)

                    def split_gates(c):
                        dve.wait_ge(s_gt, c + 1)
                        dve.tensor_copy(gh[:, :], ps_gT).then_inc(s_gth, 1)
                        dve.wait_ge(s_gth, c + 1)
                        dve.tensor_tensor(gl[:, :], ps_gT, gh[:, :].bitcast(F32), ALU.subtract).then_inc(s_gtc, 1)

                    def combine(c, e):
                        dve.wait_ge(s_gb, c * E + e + 1)
                        dve.wait_ge(s_y, c * E + e + 1)
                        y_e = yb[:, bass.ds((c & 1) * E + e, 1), :]
                        if e == 0:
                            dve.wait_ge(s_new, c + 1)
                            dve.tensor_tensor(acc[:, :].unsqueeze(1), y_e, ps_gate[e % 2].unsqueeze(1), ALU.mult).then_inc(s_prod, 1)
                            return
                        if e > 2:
                            dve.wait_ge(s_acc, c * (E - 1) + e - 2)
                        dve.tensor_tensor(prod[:, e % 2, :].unsqueeze(1), y_e, ps_gate[e % 2].unsqueeze(1), ALU.mult).then_inc(s_prod, 1)
                        dve.wait_ge(s_prod, AHEAD + c * E + e + 1)
                        if e > 1:
                            dve.wait_ge(s_acc, c * (E - 1) + e - 1)
                        dve.tensor_tensor(acc[:, :], acc[:, :], prod[:, e % 2, :], ALU.add).then_inc(s_acc, 1)
                        if e == E - 1:
                            dve.wait_ge(s_acc, (c + 1) * (E - 1))
                            dve.scalar_tensor_tensor(x[:, bass.ds(c, 1), :], acc[:, :].unsqueeze(1), 0.5, x[:, bass.ds(c, 1), :],
                                                     ALU.mult, ALU.add).then_inc(s_new, 1)

                    dve.wait_ge(s_c, 16 * 5)
                    dve.tensor_copy(selr[:, :, :], sel[:, :, :]).then_inc(s_sel, 1)
                    dve.wait_ge(s_gates, 1)
                    dve.wait_ge(s_sel, 1)
                    with dve.Fori(1, NB - 1) as c:
                        gates_of(c - 1)
                        for s in range(HALF - 1, S1):
                            if s in VEC:
                                low_part(dve, c, s, s_hld)
                            if s == HALF - 1:
                                split_gates(c - 1)
                            if s >= HALF and s % 2 == 0:
                                combine(c - 1, (s - HALF) // 2)
                    gates_of(NB - 2)
                    split_gates(NB - 2)
                    for s in range(S1 + LAG + E):
                        if s in VEC:
                            low_part(dve, NB - 1, s, s_hld)
                        if 1 <= s <= E:
                            combine(NB - 2, s - 1)
                        if s == OWN_GATES - 1:
                            gates_of(NB - 1)
                        if s == OWN_GATES:
                            split_gates(NB - 1)
                        for e in range(E):
                            if s == own_step(e):
                                combine(NB - 1, e)


class Mamba:

    def __init__(self, nc, x, ones, ident, dram):
        self.nc, self.x, self.ones, self.ident, self.dram = nc, x, ones, ident, dram

    def build(self):
        nc, x, dram, ones, ident = self.nc, self.x, self.dram, self.ones, self.ident
        PAIRS = NL * NB
        with ExitStack() as ctx:
            def sb(name, shape):
                return ctx.enter_context(nc.sbuf_tensor(name, shape, F32))

            def sem(name):
                return ctx.enter_context(nc.semaphore(name))

            ps = ctx.enter_context(nc.psum_tensor("ps_m", [128, 8, 512], F32))
            ps_v = [ps[:, 2 * et:2 * et + 2, :].rearrange("p b (n t) -> p (b n) t", t=CH) for et in range(ET)]
            ps_v_half = [[ps[:, 2 * et + b, :] for b in range(2)] for et in range(ET)]
            ps_uT = ps[0:CH, 4, 0:EI]
            ps_carry = ps[0:NS, 4, EI:2 * EI]
            bank_a, bank_b, bank_c = ps[:, 5, :], ps[:, 6, :], ps[:, 7, :]
            bank_of = (bank_b, bank_c)

            a = sb("a", [D, NB, L])
            w_in = sb("w_in", [128, NW_IN])
            w_out = [sb(f"w_out{p}", [128, NW_OUT]) for p in range(2)]
            kern = sb("kern", [CH, CH])
            eps = sb("eps_m", [128, 1])
            third = sb("third", [128, 1])
            small = sb("small", [128, 1])
            decay = sb("decay", [128, 2, ET, HC, NS, CH])
            decay0 = sb("decay0", [128, 2, ET, HC, NS])
            cb = sb("cb", [128, NC, NS, CH])
            g = [sb(f"g{p}", [CH + NS, NS, CH]) for p in range(2)]
            su = [sb(f"su{p}", [CH + NS, EI]) for p in range(2)]
            h = [sb(f"h{k}", [128, NS, CH]) for k in range(4)]
            hc = [sb(f"hc{k}", [128, NS, CH]) for k in range(4)]
            carry_in = sb("carry_in", [128, 2, NS])
            sq = sb("sq_m", [D, L])
            rs = sb("rs_m", [D, L])
            xr = sb("xr", [D, L])
            cv = [sb(f"cv{et}", [128, KC - 1 + L]) for et in range(ET)]
            conv = [sq, rs]
            sig = [sb(f"sig{et}", [128, L]) for et in range(ET)]
            xb = [sb(f"xb{p}", [128, ET, L]) for p in range(2)]
            sz = [sb(f"sz{p}", [128, ET, L]) for p in range(2)]
            u = [sb(f"u{p}", [128, ET, L]) for p in range(2)]
            bt = [sb(f"bt{p}", [CH, NC, NS]) for p in range(2)]
            dtc = sb("dtc", [CH + NS, L])
            dtr, csb, zeros = dtc[0:R, :], dtc[32:32 + NS, :], dtc[CH:CH + NS, 0:EI]
            mag, ex, lg = sq, rs, xr
            delta = sb("delta", [128, ET, L])
            aexp = sb("aexp", [128, ET * NS])
            aneg = [sb(f"aneg{p}", [128, ET * NS]) for p in range(2)]
            y = u
            ln_x, ln_sq, ln_rs = (lambda c, t=t: t[c // ET][:, c % ET, :] for t in (u, sz, xb))

            s_c = sem("m_constants_loaded")
            s_init = sem("m_fills_done")
            s_eps = sem("m_eps_filled")
            s_wi = sem("m_in_weights_loaded")
            s_wo = [sem(f"m_out_weights{p}_loaded") for p in range(2)]
            s_mean = sem("m_mean_ready")
            s_lnx = sem("m_centred_ready")
            s_lnsq = sem("m_ln_squares_ready")
            s_lnvar = sem("m_ln_variance_ready")
            s_lnlog = sem("m_ln_log_ready")
            s_lnrs = sem("m_ln_rstd_ready")
            s_a = sem("m_layernorm_ready")
            s_sq = sem("m_squares_ready")
            s_ms = sem("m_mean_square_ready")
            s_log = sem("m_log_ready")
            s_rs = sem("m_rstd_ready")
            s_xr = sem("m_normed_ready")
            s_xi = sem("m_inner_product_ready")
            s_cv = sem("m_inner_copied")
            s_z = sem("m_gate_product_ready")
            s_zc = sem("m_gate_copied")
            s_zs = sem("m_gate_sigmoid_step")
            s_zsig = sem("m_gate_sigmoid_ready")
            s_sz = sem("m_gate_silu_ready")
            s_tap0 = sem("m_conv_first_tap")
            s_cd = sem("m_conv_step")
            s_cst = sem("m_conv_sigmoid_step")
            s_cs = sem("m_conv_sigmoid_ready")
            s_xb = sem("m_inner_silu_ready")
            s_dc = sem("m_dt_c_products_ready")
            s_bp = sem("m_b_products_ready")
            s_xpc = sem("m_x_products_copied")
            s_dtp = sem("m_dt_product_ready")
            s_mag = sem("m_dt_magnitude_ready")
            s_ex = sem("m_dt_exp_ready")
            s_pm = sem("m_log1p_start_ready")
            s_sp = sem("m_dt_log_and_relu_ready")
            s_sd = sem("m_softplus_step")
            s_delta = sem("m_delta_ready")
            s_u = sem("m_u_ready")
            s_al = sem("m_a_exp_ready")
            s_an = sem("m_a_ready")
            s_da = sem("m_decay_ready")
            s_d0 = sem("m_decay0_ready")
            s_d0c = sem("m_decay0_copied")
            s_cs_st = sem("m_c_stored")
            s_cb = [sem(f"m_c{c}_spread") for c in range(NC)]
            s_g = sem("m_kernel_ready")
            s_uT = sem("m_uT_ready")
            s_ca = sem("m_carry_product_ready")
            s_su = sem("m_scan_inputs_ready")
            s_v = sem("m_v_ready")
            s_ci = sem("m_carry_in_ready")
            s_cad = sem("m_carry_added")
            s_scan = sem("m_scan_done")
            s_hc = sem("m_hc_ready")
            s_y = sem("m_y_reduced")
            s_yd = sem("m_y_skip_added")
            s_yg = sem("m_y_gated")
            s_op = sem("m_out_product_ready")
            s_res = sem("m_residual_added")
            s_end = sem("m_x_updated")
            s_passed = {name: sem(f"m_wait_passed_{name}") for name in ("pe", "pool", "sp", "dve")}

            def wi(name, k=0, n=1, rows=128):
                at = COL_IN[name] + k
                return w_in[0:rows, at:at + n]

            def wo(p, name, k=0, n=1):
                at = COL_OUT[name] + k
                return w_out[p][:, at:at + n]

            def is0(i):
                return isinstance(i, int) and i == 0

            def pairs(eng, prologue, slot, epilogue):
                def body(i, p, prev, more):
                    for c in range(NC):
                        for et in range(ET):
                            slot(i, p, c, et, prev, more)

                prologue()
                body(0, 0, False, True)
                with eng.Fori(0, PAIRS // 2 - 1) as j:
                    body(j * 2 + 1, 1, True, True)
                    body(j * 2 + 2, 0, True, True)
                body(PAIRS - 1, 1, True, False)
                epilogue()

            with nc.Block() as block:
                @block.sync
                def _(sp):
                    sp.dma_start(kern[:, :], dram["kern"]).then_inc(s_c, 16)
                    for p in range(2):
                        sp.dma_start(g[p][CH:CH + NS, :, :], dram["carry_kern"]).then_inc(s_c, 16)

                    def layer_of(t, i):
                        layer = (i // NB) & (NL - 1)
                        if isinstance(layer, int):
                            return dram[t][layer, :, :]
                        return dram[t][bass.ds(layer, 1), :, :].rearrange("o p n -> (o p) n")

                    def load_in(i):
                        if not is0(i):
                            sp.wait_ge(s_sp, i * ET * 2)
                            sp.sem_inc(s_passed["sp"], 1)
                        sp.dma_start(w_in[:, :], layer_of("w_in", i)).then_inc(s_wi, 16)

                    def load_out(i, p):
                        if not (isinstance(i, int) and i < 2):
                            sp.wait_ge(s_res, i - 1)
                            sp.sem_inc(s_passed["sp"], 1)
                        sp.dma_start(w_out[p][:, :], layer_of("w_out", i)).then_inc(s_wo[p], 16)

                    def store_c(i):
                        sp.wait_ge(s_xpc, i * 3 + 2)
                        sp.sem_inc(s_passed["sp"], 1)
                        if not is0(i):
                            for k in range(NC):
                                sp.wait_ge(s_cb[k], i * 16)
                        sp.dma_start(dram["c_scratch"].rearrange("c n t -> n c t"),
                                     csb.rearrange("n (c t) -> n c t", t=CH)).then_inc(s_cs_st, 16)
                        sp.wait_ge(s_cs_st, i * 16 + 16)
                        sp.sem_inc(s_passed["sp"], 1)

                    def spread_c(i, k):
                        if not is0(i):
                            sp.wait_ge(s_hc, (i - 1) * UN + ET * (k + 1))
                        sp.dma_start(cb[:, k, :, :], dram["c_scratch"][k:k + 1, :, :].broadcast_to([128, NS, CH]))\
                          .then_inc(s_cb[k], 16)

                    def prologue():
                        load_in(0)
                        load_out(0, 0)
                        store_c(0)
                        load_in(1)
                        for k in range(NC):
                            spread_c(0, k)

                    def slot(i, p, c, et, prev, more):
                        if more and c == NC - 1 and et == 1:
                            load_out(i + 1, 1 - p)
                            store_c(i + 1)
                            for k in range(NC - 2):
                                spread_c(i + 1, k)
                            load_in(i + 2)
                            for k in range(NC - 2, NC):
                                spread_c(i + 1, k)

                    pairs(sp, prologue, slot, lambda: None)

                @block.tensor
                def _(pe):
                    def mean_square(i):
                        pe.wait_ge(s_sq, i + 1)
                        pe.matmul(bank_a, ones[:, :], sq[:, :], start=True, stop=True).then_inc(s_ms, 1)

                    def inner_product(i, et):
                        pe.wait_ge(s_wi, i * 16 + 16)
                        pe.wait_ge(s_xr, i + 1)
                        pe.matmul(bank_of[et], wi("in_w", et * 128, 128), xr[:, :], start=True, stop=True).then_inc(s_xi, 1)

                    def gate_product(i, et):
                        pe.wait_ge(s_cv, i * ET + et + 1)
                        pe.matmul(bank_of[et], wi("in_w", EI + et * 128, 128), xr[:, :], start=True, stop=True).then_inc(s_z, 1)

                    def dt_c_product(i, p, et):
                        pe.wait_ge(s_xb, i * ET + et + 1)
                        if et == 0:
                            pe.wait_ge(s_zc, i * ET + 1)
                        pe.matmul(bank_b[0:32 + NS, :], wi("xp", et * XW, 32 + NS), xb[p][:, et, :], start=(et == 0), stop=(et == ET - 1))\
                          .then_inc(s_dc, 1)

                    def b_products(i, p):
                        for k in range(NC):
                            for et in range(ET):
                                mm = pe.matmul(bank_a[0:CH, k * NS:(k + 1) * NS], xb[p][:, et, k * CH:(k + 1) * CH],
                                               wi("xp", et * XW + 32 + NS, NS), start=(et == 0), stop=(et == ET - 1))
                        mm.then_inc(s_bp, 1)

                    def dt_product(i, et):
                        pe.wait_ge(s_xpc, i * 3 + 2)
                        pe.wait_ge(s_zc, i * ET + ET)
                        pe.matmul(bank_of[et], wi("dt_w", et * 128, 128, R), dtr, start=True, stop=True).then_inc(s_dtp, 1)

                    def transposes(i, p, c):
                        if not (is0(i) and c == 0):
                            pe.wait_ge(s_su, i * NC + c)
                        if c == 0:
                            pe.wait_ge(s_u, i * ET + ET)
                        pe.sem_inc(s_passed["pe"], 1)
                        for et in range(ET):
                            mm = pe.transpose(ps_uT[:, et * 128:(et + 1) * 128], u[p][:, et, c * CH:(c + 1) * CH], ident[:, :])
                        mm.then_inc(s_uT, 1)

                    def out_product(i, p, et):
                        pe.wait_ge(s_yg, i * ET + et + 1)
                        pe.matmul(bank_a, wo(p, "out_w", et * D, D), sz[p][:, et, :], start=(et == 0), stop=(et == ET - 1))\
                          .then_inc(s_op, 1)

                    def prologue():
                        for c in range(NB):
                            pe.matmul(ps[:, c, :], ones[:, :], x[:, c, :], start=True, stop=True).then_inc(s_mean, 1)
                        for c in range(NB):
                            pe.wait_ge(s_lnsq, c + 1)
                            pe.matmul(ps[:, c, :], ones[:, :], ln_sq(c), start=True, stop=True).then_inc(s_lnvar, 1)
                            if c == 0:
                                mean_square(0)
                        for et in range(ET):
                            inner_product(0, et)
                        for et in range(ET):
                            gate_product(0, et)
                        for et in range(ET):
                            dt_c_product(0, 0, et)
                        b_products(0, 0)
                        for et in range(ET):
                            dt_product(0, et)
                        transposes(0, 0, 0)
                        pe.wait_ge(s_xpc, 3)
                        mean_square(1)

                    def slot(i, p, c, et, prev, more):
                        k, n = c * ET + et, i + 1
                        q = i * NC + c
                        if et == 0:
                            pe.wait_ge(s_su, q + 1)
                            pe.wait_ge(s_g, q + 1)
                            if c < NC - 1:
                                transposes(i, p, c + 1)
                                pe.matmul(ps_carry, g[c % 2][:, :, CH - 1], su[c % 2][:, :], start=True, stop=True).then_inc(s_ca, 1)
                            elif more:
                                transposes(n, 1 - p, 0)
                        if not (is0(i) and c == 0):
                            pe.wait_ge(s_scan, (q - 1) * ET + et + 1)
                        for b in range(2):
                            mm = pe.matmul(ps_v_half[et][b], su[c % 2][:, et * 128:(et + 1) * 128],
                                           g[c % 2][:, b * NS // 2:(b + 1) * NS // 2, :], start=True, stop=True)
                        mm.then_inc(s_v, 1)
                        if more and k in (0, 1):
                            inner_product(n, k)
                        if more and k in (4, 5):
                            gate_product(n, k - 4)
                        if prev and k in (2, 3):
                            out_product(i - 1, 1 - p, k - 2)
                        if more and k in (6, 7):
                            dt_c_product(n, 1 - p, k - 6)
                        if more and k in (8, 9):
                            dt_product(n, k - 8)
                        if more and k == 10:
                            if prev:
                                pe.wait_ge(s_res, i)
                            b_products(n, 1 - p)
                        if more and k == 14:
                            pe.wait_ge(s_xpc, n * 3 + 3)
                            mean_square(n + 1)

                    pairs(pe, prologue, slot, lambda: [out_product(PAIRS - 1, 1, et) for et in range(ET)])

                @block.scalar
                def _(act):
                    def squares(i):
                        if not is0(i):
                            act.wait_ge(s_delta, i * ET)
                        if not (isinstance(i, int) and i < NB):
                            act.wait_ge(s_res, i - NB + 1 if isinstance(i, int) else i - 2)
                        act.activation(sq[:, :].unsqueeze(1), a[:, bass.ds(i & (NB - 1), 1), :], ACT.Square).then_inc(s_sq, 1)

                    def rstd(i):
                        act.wait_ge(s_ms, i + 1)
                        act.activation(rs[:, :], bank_a, ACT.Ln, bias=eps[:, 0:1]).then_inc(s_log, 1)
                        act.wait_ge(s_log, i + 1)
                        act.activation(rs[:, :], rs[:, :], ACT.Exp, scale=-0.5).then_inc(s_rs, 1)

                    def copy_inner(i, et):
                        act.wait_ge(s_xi, i * ET + et + 1)
                        act.activation(cv[et][:, KC - 1:KC - 1 + L], bank_of[et], ACT.Copy).then_inc(s_cv, 1)

                    def first_tap(i, et):
                        act.wait_ge(s_cv, i * ET + et + 1)
                        if et == 0 and not is0(i):
                            act.wait_ge(s_xb, i * ET)
                        act.activation(conv[et][:, :], cv[et][:, 0:L], ACT.Identity, scale=wi("conv_w", et * KC), bias=wi("conv_b", et))\
                           .then_inc(s_tap0, 1)

                    def a_exp(i):
                        act.wait_ge(s_wi, i * 16 + 16)
                        act.activation(aexp[:, :], wi("a_log", 0, ET * NS), ACT.Exp).then_inc(s_al, 1)

                    def sigmoid(dst, src, step, count):
                        act.activation(dst, src, ACT.Exp, scale=-1.0).then_inc(step, 1)
                        act.wait_ge(step, count + 1)
                        act.activation(dst, dst, ACT.Ln, bias=1.0).then_inc(step, 1)
                        act.wait_ge(step, count + 2)
                        return act.activation(dst, dst, ACT.Exp, scale=-1.0)

                    def conv_sigmoid(i, et):
                        act.wait_ge(s_cd, (i * ET + et + 1) * (KC - 1))
                        sigmoid(sig[et][:, :], conv[et][:, :], s_cst, (i * ET + et) * 2).then_inc(s_cs, 1)

                    def copy_gate(i, p, et, prev):
                        if prev:
                            act.wait_ge(s_op, (i - 1) * ET)
                        act.wait_ge(s_z, i * ET + et + 1)
                        act.activation(sz[p][:, et, :], bank_of[et], ACT.Copy).then_inc(s_zc, 1)

                    def gate_sigmoid(i, p, et):
                        act.wait_ge(s_zc, i * ET + et + 1)
                        sigmoid(sig[et][:, :], sz[p][:, et, :], s_zs, (i * ET + et) * 2).then_inc(s_zsig, 1)

                    def copy_x_products(i, p):
                        act.wait_ge(s_dc, i * ET + ET)
                        act.activation(dtr, bank_b[0:R, :], ACT.Copy).then_inc(s_xpc, 1)
                        if not is0(i):
                            act.wait_ge(s_cs_st, i * 16)
                        act.activation(csb, bank_b[32:32 + NS, :], ACT.Copy).then_inc(s_xpc, 1)

                    def copy_b(i, p):
                        act.wait_ge(s_bp, i + 1)
                        act.activation(bt[p][:, :, :], bank_a[0:CH, 0:NC * NS].rearrange("p (c n) -> p c n", n=NS), ACT.Copy)\
                           .then_inc(s_xpc, 1)

                    def softplus(i, et):
                        act.wait_ge(s_dtp, i * ET + et + 1)
                        if et:
                            act.wait_ge(s_delta, i * ET + et)
                        act.activation(mag[:, :], bank_of[et], ACT.Abs, bias=wi("dt_b", et)).then_inc(s_mag, 1)
                        act.wait_ge(s_mag, i * ET + et + 1)
                        act.activation(ex[:, :], mag[:, :], ACT.Exp, scale=-1.0).then_inc(s_ex, 1)
                        act.wait_ge(s_ex, i * ET + et + 1)
                        act.activation(mag[:, :], ex[:, :], ACT.Identity, scale=-1.0 / 4, bias=third[:, 0:1]).then_inc(s_pm, 1)
                        if not is0(i):
                            act.wait_ge(s_sz, (i - 1) * ET + et + 1)
                        act.activation(sig[et][:, :], ex[:, :], ACT.Relu, scale=-1.0, bias=small[:, 0:1]).then_inc(s_pm, 1)
                        act.activation(lg[:, :], ex[:, :], ACT.Ln, bias=1.0).then_inc(s_sp, 1)
                        if et == 0 and not is0(i):
                            act.wait_ge(s_da, i * 2 * ET * NS)
                            act.wait_ge(s_u, i * ET)
                        act.activation(delta[:, et, :], bank_of[et], ACT.Relu, bias=wi("dt_b", et)).then_inc(s_sp, 1)

                    def decays(i, p, half, first, last):
                        for m in range(first, last):
                            et, n = m // NS, m % NS
                            act.activation(decay[:, half, et, :, n, :],
                                           delta[:, et, half * L // 2:(half + 1) * L // 2].rearrange("p (c t) -> p c t", t=CH),
                                           ACT.Exp, scale=aneg[p][:, m:m + 1]).then_inc(s_da, 1)

                    def scan_inputs(i, p, c):
                        act.wait_ge(s_uT, i * NC + c + 1)
                        if c:
                            act.wait_ge(s_ca, i * (NC - 1) + c)
                        if not (is0(i) and c < 2):
                            act.wait_ge(s_v, (i * NC + c - 1) * ET)
                        act.activation(su[c % 2][0:CH, :], ps_uT, ACT.Copy)
                        carried = zeros if c == 0 else ps_carry
                        act.activation(su[c % 2][CH:CH + NS, :], carried, ACT.Copy).then_inc(s_su, 1)

                    def prologue():
                        act.preload_act_table_set(TABLES)
                        act.wait_ge(s_init, 3)
                        act.wait_ge(s_eps, 3)
                        def ln_squares(c):
                            act.wait_ge(s_lnx, c + 1)
                            act.activation(ln_sq(c), ln_x(c), ACT.Square).then_inc(s_lnsq, 1)

                        def ln_rstd(first, last):
                            for c in range(first, last):
                                act.wait_ge(s_lnvar, c + 1)
                                act.activation(ln_rs(c), ps[:, c, :], ACT.Ln, bias=eps[:, 0:1]).then_inc(s_lnlog, 1)
                            for c in range(first, last):
                                act.wait_ge(s_lnlog, c + 1)
                                act.activation(ln_rs(c), ln_rs(c), ACT.Exp, scale=-0.5).then_inc(s_lnrs, 1)

                        ln_squares(0)
                        ln_rstd(0, 1)
                        act.wait_ge(s_a, 1)
                        squares(0)
                        for c in range(1, NB):
                            ln_squares(c)
                        rstd(0)
                        for et in range(ET):
                            copy_inner(0, et)
                        for et in range(ET):
                            first_tap(0, et)
                        ln_rstd(1, NB)
                        a_exp(0)
                        for et in range(ET):
                            conv_sigmoid(0, et)
                        act.wait_ge(s_a, NB)
                        for et in range(ET):
                            copy_gate(0, 0, et, False)
                        copy_x_products(0, 0)
                        copy_b(0, 0)
                        softplus(0, 0)
                        act.wait_ge(s_an, 1)
                        act.wait_ge(s_delta, 1)
                        decays(0, 0, 0, 0, NS)
                        softplus(0, 1)
                        scan_inputs(0, 0, 0)
                        squares(1)
                        act.wait_ge(s_delta, ET)
                        decays(0, 0, 0, NS, ET * NS)
                        rstd(1)

                    second = [8, 5, 8, 3, 3, 5]
                    first = {11: 8, 12: 8, 13: 8, 14: 8}

                    def slot(i, p, c, et, prev, more):
                        k, n = c * ET + et, i + 1
                        if et == 0:
                            if c < NC - 1:
                                scan_inputs(i, p, c + 1)
                            elif more:
                                scan_inputs(n, 1 - p, 0)
                        if more and k in (1, 2):
                            copy_inner(n, k - 1)
                            first_tap(n, k - 1)
                        if more and k in (3, 4):
                            conv_sigmoid(n, k - 3)
                        if more and k in (5, 6):
                            copy_gate(n, 1 - p, k - 5, prev)
                        if more and k == 5:
                            a_exp(n)
                        if more and k == 8:
                            copy_x_products(n, 1 - p)
                        if k in (7, 8):
                            if more:
                                act.wait_ge(s_xb, n * ET + k - 7 + 1)
                            gate_sigmoid(i, p, k - 7)
                        if more and k in (9, 10):
                            softplus(n, k - 9)
                        if more and k == 11:
                            copy_b(n, 1 - p)
                        if k < len(second):
                            if k == 0 and not is0(i):
                                act.wait_ge(s_scan, i * UN)
                            decays(i, p, 1, sum(second[:k]), sum(second[:k + 1]))
                        if more and k in first:
                            if k == 11:
                                act.wait_ge(s_an, n + 1)
                                act.wait_ge(s_scan, i * UN + UN // 2)
                            done = sum(v for s, v in first.items() if s < k)
                            act.wait_ge(s_delta, n * ET + 1 + done // NS)
                            decays(n, 1 - p, 0, done, done + first[k])
                        if more and k == 12:
                            squares(n + 1)
                        if more and k == 15:
                            rstd(n + 1)

                    pairs(act, prologue, slot, lambda: None)

                @block.gpsimd
                def _(pool):
                    def kernel_of(i, p, c):
                        if c == 0:
                            pool.wait_ge(s_xpc, i * 3 + 3)
                        if not (is0(i) and c < 2):
                            pool.wait_ge(s_v, (i * NC + c - 1) * ET)
                        if c > 1:
                            pool.wait_ge(s_ca, i * (NC - 1) + c - 1)
                        elif c == 0 and not is0(i):
                            pool.wait_ge(s_ca, i * (NC - 1))
                        pool.tensor_tensor(g[c % 2][0:CH, :, :], kern[:, :].unsqueeze(1).broadcast_to([CH, NS, CH]),
                                           bt[p][:, c, :].unsqueeze(2).broadcast_to([CH, NS, CH]), ALU.mult).then_inc(s_g, 1)

                    def first_decays(i, half):
                        pool.wait_ge(s_da, (i * 2 + half + 1) * ET * NS)
                        pool.sem_inc(s_passed["pool"], 1)
                        d0 = decay[:, half, :, :, :, 0].rearrange("p e c n -> p (e c n)")
                        pool.tensor_copy(decay0[:, half, :, :, :].rearrange("p e c n -> p (e c n)"), d0).then_inc(s_d0c, 1)
                        pool.wait_ge(s_d0c, i * 2 + half + 1)
                        pool.sem_inc(s_passed["pool"], 1)
                        pool.memset(d0, 0.0).then_inc(s_d0, 1)

                    def times_c(i, c, et):
                        if et == 0:
                            pool.wait_ge(s_cb[c], i * 16 + 16)
                        pool.wait_ge(s_scan, (i * NC + c) * ET + et + 1)
                        if not (is0(i) and c < 2):
                            pool.wait_ge(s_y, (i * NC + c - 2) * ET + et + 1)
                        pool.tensor_tensor(hc[(c % 2) * ET + et][:, :, :], h[(c % 2) * ET + et][:, :, :], cb[:, c, :, :], ALU.mult).then_inc(s_hc, 1)

                    def prologue():
                        pool.memset(zeros, 0.0).then_inc(s_init, 1)
                        pool.wait_ge(s_init, 1)
                        for et in range(ET):
                            pool.memset(cv[et][:, 0:KC - 1], 0.0).then_inc(s_init, 1)
                        pool.wait_ge(s_c, 16 * 3)
                        kernel_of(0, 0, 0)
                        kernel_of(0, 0, 1)
                        first_decays(0, 0)

                    def slot(i, p, c, et, prev, more):
                        if et == 1:
                            if c < NC - 2:
                                kernel_of(i, p, c + 2)
                            elif more:
                                kernel_of(i + 1, 1 - p, c + 2 - NC)
                        if c * ET + et == 6:
                            first_decays(i, 1)
                        times_c(i, c, et)
                        if et == 0 and c == NC - 1 and more:
                            first_decays(i + 1, 0)

                    pairs(pool, prologue, slot, lambda: None)

                @block.vector
                def _(dve):
                    def normed(i):
                        dve.wait_ge(s_rs, i + 1)
                        dve.wait_ge(s_wi, i * 16 + 16)
                        dve.scalar_tensor_tensor(xr[:, :].unsqueeze(1), a[:, bass.ds(i & (NB - 1), 1), :], wi("norm_w"),
                                                 rs[:, :].unsqueeze(1), ALU.mult, ALU.mult).then_inc(s_xr, 1)

                    def convolution(i, et):
                        def tap(k):
                            def op():
                                if k == 1:
                                    dve.wait_ge(s_tap0, i * ET + et + 1)
                                else:
                                    dve.wait_ge(s_cd, (i * ET + et) * (KC - 1) + k - 1)
                                dve.scalar_tensor_tensor(conv[et][:, :], cv[et][:, k:k + L], wi("conv_w", et * KC + k), conv[et][:, :],
                                                         ALU.mult, ALU.add).then_inc(s_cd, 1)
                            return op
                        return [tap(k) for k in range(1, KC)]

                    def inner_silu(i, p, et):
                        dve.wait_ge(s_cs, i * ET + et + 1)
                        dve.tensor_tensor(xb[p][:, et, :], conv[et][:, :], sig[et][:, :], ALU.mult).then_inc(s_xb, 1)

                    def gate_silu(i, p, et):
                        dve.wait_ge(s_zsig, i * ET + et + 1)
                        dve.tensor_tensor(sz[p][:, et, :], sz[p][:, et, :], sig[et][:, :], ALU.mult).then_inc(s_sz, 1)

                    def negative_a(i, p):
                        dve.wait_ge(s_al, i + 1)
                        if not (isinstance(i, int) and i < 2):
                            dve.wait_ge(s_da, (i - 1) * 2 * ET * NS)
                        dve.tensor_scalar(aneg[p][:, :], aexp[:, :], -1.0, None, ALU.mult).then_inc(s_an, 1)

                    def softplus(i, p, et):
                        n = (i * ET + et) * 4

                        def power2():
                            dve.wait_ge(s_pm, (i * ET + et) * 2 + 1)
                            dve.tensor_tensor(mag[:, :], mag[:, :], ex[:, :], ALU.mult).then_inc(s_sd, 1)

                        def power1():
                            dve.wait_ge(s_sd, n + 1)
                            dve.scalar_tensor_tensor(mag[:, :], mag[:, :], -0.5, ex[:, :], ALU.add, ALU.mult).then_inc(s_sd, 1)

                        def power0():
                            dve.wait_ge(s_sd, n + 2)
                            dve.scalar_tensor_tensor(mag[:, :], mag[:, :], 1.0, ex[:, :], ALU.add, ALU.mult).then_inc(s_sd, 1)

                        def choose():
                            dve.wait_ge(s_sd, n + 3)
                            dve.wait_ge(s_sp, (i * ET + et) * 2 + 1)
                            dve.sem_inc(s_passed["dve"], 1)
                            dve.copy_predicated(lg[:, :], sig[et][:, :].bitcast(mybir.dt.uint32), mag[:, :]).then_inc(s_sd, 1)

                        def add_relu():
                            dve.wait_ge(s_sd, n + 4)
                            dve.wait_ge(s_sp, (i * ET + et) * 2 + 2)
                            dve.tensor_tensor(delta[:, et, :], delta[:, et, :], lg[:, :], ALU.add).then_inc(s_delta, 1)

                        def times_x():
                            dve.wait_ge(s_delta, i * ET + et + 1)
                            dve.tensor_tensor(u[p][:, et, :], delta[:, et, :], xb[p][:, et, :], ALU.mult).then_inc(s_u, 1)

                        return [power2, power1, power0, choose, add_relu, times_x]

                    def reduce_states(i, p, k):
                        c, et = k // ET, k % ET
                        dve.wait_ge(s_hc, (i * NC + c) * ET + et + 1)
                        dve.tensor_reduce(y[p][:, et, c * CH:(c + 1) * CH], hc[(c % 2) * ET + et][:, :, :].rearrange("p n t -> p t n"),
                                          AX.X, ALU.add).then_inc(s_y, 1)

                    def gated_output(i, p):
                        for et in range(ET):
                            dve.wait_ge(s_y, (i * NC + NC - 1) * ET + et + 1)
                            dve.wait_ge(s_wo[p], (i // 2) * 16 + 16 if isinstance(i, int) else (i >> 1) * 16 + 16)
                            dve.scalar_tensor_tensor(xb[p][:, et, :], xb[p][:, et, :], wo(p, "dp", et), y[p][:, et, :], ALU.mult, ALU.add)\
                               .then_inc(s_yd, 1)
                        for et in range(ET):
                            dve.wait_ge(s_yd, i * ET + et + 1)
                            dve.tensor_tensor(sz[p][:, et, :], xb[p][:, et, :], sz[p][:, et, :], ALU.mult).then_inc(s_yg, 1)

                    def residual(i):
                        dve.wait_ge(s_op, i * ET + ET)
                        at = bass.ds(i & (NB - 1), 1)
                        dve.tensor_tensor(a[:, at, :], a[:, at, :], bank_a.unsqueeze(1), ALU.add).then_inc(s_res, 1)

                    BEHIND = 2
                    CONV_SLOTS = (2, 3)
                    PLUS_SLOTS = (9, 10, 11, 12)

                    def prologue():
                        dve.memset(eps[:, :], EPS).then_inc(s_eps, 1)
                        dve.memset(third[:, :], 1.0 / 3).then_inc(s_eps, 1)
                        dve.memset(small[:, :], SMALL).then_inc(s_eps, 1)
                        for c in range(NB):
                            dve.wait_ge(s_mean, c + 1)
                            dve.tensor_tensor(ln_x(c), x[:, c, :], ps[:, c, :], ALU.subtract).then_inc(s_lnx, 1)
                        def normalise(c):
                            dve.wait_ge(s_lnx, c + 1)
                            dve.wait_ge(s_lnrs, c + 1)
                            dve.tensor_tensor(a[:, c, :], ln_x(c), ln_rs(c), ALU.mult).then_inc(s_a, 1)

                        normalise(0)
                        dve.wait_ge(s_a, 1)
                        normed(0)
                        for et in range(ET):
                            for op in convolution(0, et):
                                op()
                        for c in range(1, NB):
                            normalise(c)
                        dve.wait_ge(s_a, NB)
                        negative_a(0, 0)
                        for et in range(ET):
                            inner_silu(0, 0, et)
                        for et in range(ET):
                            for op in softplus(0, 0, et):
                                op()
                        normed(1)

                    def slot(i, p, c, et, prev, more):
                        k, n = c * ET + et, i + 1
                        un = i * UN + k
                        half, ch = c // HC, c % HC
                        carries = i * (UN - ET) + k - ET
                        between = []
                        if more and k in CONV_SLOTS:
                            between = convolution(n, CONV_SLOTS.index(k))
                        if more and k in PLUS_SLOTS:
                            between = softplus(n, 1 - p, PLUS_SLOTS.index(k) // 2)
                            between = between[:3] if PLUS_SLOTS.index(k) % 2 == 0 else between[3:]

                        def step_between():
                            if between:
                                between.pop(0)()

                        if c:
                            dve.wait_ge(s_ci, carries + 1)
                            dve.wait_ge(s_v, un + 1)
                            dve.tensor_tensor(ps_v[et][:, :, 0], ps_v[et][:, :, 0], carry_in[:, et, :], ALU.add).then_inc(s_cad, 1)
                        step_between()
                        if ET <= k + 1 < UN:
                            c2, e2 = (k + 1) // ET, (k + 1) % ET
                            if k + 1 == UN // 2:
                                dve.wait_ge(s_d0, i * 2 + 2)
                            dve.wait_ge(s_scan, un)
                            dve.tensor_tensor(carry_in[:, e2, :], decay0[:, c2 // HC, e2, c2 % HC, :], h[(k - 1) % 4][:, :, CH - 1], ALU.mult)\
                               .then_inc(s_ci, 1)
                        step_between()
                        if k >= BEHIND:
                            reduce_states(i, p, k - BEHIND)
                        elif prev:
                            reduce_states(i - 1, 1 - p, UN + k - BEHIND)
                        if c:
                            dve.wait_ge(s_cad, carries + 1)
                        step_between()
                        if k % (UN // 2) == 0:
                            dve.wait_ge(s_d0, i * 2 + half + 1)
                        dve.wait_ge(s_v, un + 1)
                        if not (is0(i) and c < 2):
                            dve.wait_ge(s_hc, un - 3)
                        dve.tensor_tensor_scan(h[k % 4][:, :, :].rearrange("p n t -> p (n t)"),
                                               decay[:, half, et, ch, :, :].rearrange("p n t -> p (n t)"),
                                               ps_v[et].rearrange("p n t -> p (n t)"), 0.0, ALU.mult, ALU.add).then_inc(s_scan, 1)
                        while between:
                            step_between()
                        if prev and k == BEHIND - 1:
                            gated_output(i - 1, 1 - p)
                        if prev and k == 4:
                            residual(i - 1)
                        if more and k in (4, 5):
                            inner_silu(n, 1 - p, k - 4)
                        if more and k == 6:
                            negative_a(n, 1 - p)
                        if k in (8, 9):
                            gate_silu(i, p, k - 8)
                        if more and k == 15:
                            if not (isinstance(i, int) and i == PAIRS - 2):
                                normed(n + 1)

                    def epilogue():
                        for k in range(UN - BEHIND, UN):
                            reduce_states(PAIRS - 1, 1, k)
                        gated_output(PAIRS - 1, 1)
                        residual(PAIRS - 1)
                        dve.wait_ge(s_res, PAIRS)
                        dve.tensor_tensor(x[:, :, :], x[:, :, :], a[:, :, :], ALU.add).then_inc(s_end, 1)
                        dve.wait_ge(s_end, 1)

                    pairs(dve, prologue, slot, epilogue)


def macaron(nc, dram):
    with ExitStack() as ctx:
        x = ctx.enter_context(nc.sbuf_tensor("x_res", [D, NB, L], F32))
        ones = ctx.enter_context(nc.sbuf_tensor("ones", [128, 128], F32))
        ident = ctx.enter_context(nc.sbuf_tensor("ident", [128, 128], F32))
        Ffn(nc, x, ones, ident, dram["x"], None, dram, "f1").build()
        Mamba(nc, x, ones, ident, dram).build()
        Ffn(nc, x, ones, ident, None, dram["out"], dram, "f2").build()


def kernel(**inputs):
    import concourse.bacc as _bacc
    from concourse.bass_utils import run_bass_kernel_spmd as _run

    f = {k.replace("L0_attn_", "m_").replace("L0_ffn_", "f_"): np.asarray(v) for k, v in inputs.items()}
    lay = np.ascontiguousarray
    arrays = {
        "x": lay(f["m_x"].reshape(NB, L, D).transpose(2, 0, 1)),
        "w1": lay(f["f_W1"].reshape(E, D, FT, 128).transpose(1, 0, 2, 3).reshape(D, S1, 128)),
        "w2": lay(f["f_W2"].reshape(E, FT, 128, D).transpose(2, 0, 1, 3).reshape(128, S1, D)),
        "b1": lay(f["f_b1"].reshape(S1, 128).T),
        "b2": lay(f["f_b2"].T),
        "wr": lay(f["f_Wr"]),
        "br": lay(np.broadcast_to(f["f_br"][None, :], (128, E))),
    }
    def tiles(v):
        return v.reshape(NL, ET, 128, -1).transpose(0, 2, 1, 3).reshape(NL, 128, -1)

    xp = f["m_x_proj_w"].transpose(0, 2, 1)
    dt_w = np.zeros((NL, 128, EI), np.float32)
    dt_w[:, :R, :] = f["m_dt_w"].transpose(0, 2, 1)
    parts = {
        "in_w": f["m_in_proj_w"].transpose(0, 2, 1),
        "xp": tiles(np.concatenate([xp[:, :, :R], np.zeros((NL, EI, 32 - R), np.float32), xp[:, :, R + NS:], xp[:, :, R:R + NS]], axis=2)),
        "out_w": tiles(f["m_out_w"].transpose(0, 2, 1)),
        "conv_w": tiles(f["m_conv_w"]),
        "conv_b": tiles(f["m_conv_b"]),
        "dt_b": tiles(f["m_dt_b"]),
        "a_log": tiles(f["m_A_log"]),
        "dp": tiles(f["m_Dp"]),
        "norm_w": f["m_norm_w"].reshape(NL, D, 1),
        "dt_w": dt_w,
    }
    arrays["w_in"] = lay(np.concatenate([parts[n] for n, _ in PACK_IN], axis=2))
    arrays["w_out"] = lay(np.concatenate([parts[n] for n, _ in PACK_OUT], axis=2))
    t = np.arange(CH)
    arrays["ones"] = np.full((128, 128), 1.0 / D, np.float32)
    arrays["ident"] = np.eye(128, dtype=np.float32)
    arrays["sel"] = lay(np.broadcast_to(np.eye(E, dtype=np.float32)[:, :, None], (E, E, 128)))
    lag = t[None, :] - t[:, None]
    arrays["kern"] = np.where(lag >= 0, BETA ** np.maximum(lag, 0).astype(np.float64), 0.0).astype(np.float32)
    arrays["carry_kern"] = (np.eye(NS)[:, :, None] * BETA ** (t + 1.0)[None, None, :]).astype(np.float32)

    nc = _bacc.Bacc("TRN2", target_bir_lowering=False, num_devices=1)
    dram = {n: nc.dram_tensor(f"in_{n}", v.shape, F32, kind="ExternalInput").ap() for n, v in arrays.items()}
    dram["out"] = nc.dram_tensor("out_x", (D, NB, L), F32, kind="ExternalOutput").ap()
    dram["c_scratch"] = nc.dram_tensor("c_scratch", (NC, NS, CH), F32, kind="Internal").ap()
    macaron(nc, dram)
    r = _run(nc, [{f"in_{n}": v for n, v in arrays.items()}], core_ids=[0])
    return lay(np.asarray(r.results[0]["out_x"]).transpose(1, 2, 0))
```
